# Optimizing a Trainium2 kernel written in Bass

```python
import numpy as np
import jax
import jax.numpy as jnp

def _softmax(x, axis=-1):
    return jax.nn.softmax(x, axis=axis)

def _gelu(x):
    return jax.nn.gelu(x, approximate=True)

def _silu(x):
    return jax.nn.silu(x)

def _sigmoid(x):
    return jax.nn.sigmoid(x)

def _layernorm(x, axis=-1, eps=1e-05):
    m = jnp.mean(x, axis=axis, keepdims=True)
    v = jnp.var(x, axis=axis, keepdims=True)
    return (x - m) / jnp.sqrt(v + eps)

def _scatter_add(tgt, idx, src, axis=0):
    return tgt.at[idx].add(src)

def _segment_sum(src, seg, n):
    return jax.ops.segment_sum(src, seg, n)
kernel_name = 'mk_seq_postln_d1_jaxref_r4_11ae71'

def setup_inputs(seed: int=0):
    np.random.seed(seed)
    _w = jnp.asarray

    def _L0_attn_setup():
        import jax, jax.numpy as jnp
        import numpy as np
        NUM_HEADS = 16
        ATT_WINDOW = 128
        GLOBAL_SIZE = 64
        key = jax.random.key(seed)
        ks = jax.random.split(key, 10)
        B, S, HID = (1, 512, 256)
        w = lambda k: jax.random.normal(k, (HID, HID), jnp.float32) * 0.02
        b = lambda k: jax.random.normal(k, (HID,), jnp.float32) * 0.02
        return {'x': jax.random.normal(ks[0], (B, S, HID), jnp.float32), 'wq': w(ks[1]), 'bq': b(ks[2]), 'wk': w(ks[3]), 'bk': b(ks[4]), 'wv': w(ks[5]), 'bv': b(ks[6]), 'wo': w(ks[7]), 'bo': b(ks[8])}
    _L0_attn_in = _L0_attn_setup()

    def _L0_ffn_setup():
        import jax, jax.numpy as jnp
        import numpy as np
        DIM = 256

        def _reference_tuple_inner(x, W_r, W_k, W_v, mu_r, mu_k):
            B, T, C = x.shape
            x_prev = jnp.concatenate([jnp.zeros((B, 1, C), x.dtype), x[:, :-1, :]], axis=1)
            xr = mu_r * x + (1.0 - mu_r) * x_prev
            xk = mu_k * x + (1.0 - mu_k) * x_prev
            r = jax.nn.sigmoid(jnp.einsum('btc,dc->btd', xr, W_r))
            k = jnp.einsum('btc,dc->btd', xk, W_k)
            k_act = jnp.square(jax.nn.relu(k))
            out = r * jnp.einsum('btc,dc->btd', k_act, W_v)
            new_state = x[:, -1, :]
            return (out, new_state)
        key = jax.random.key(seed)
        ks = jax.random.split(key, 6)
        B, T, C = (8, 512, DIM)
        x = jax.random.normal(ks[0], (B, T, C), dtype=jnp.float32)
        s = 1.0 / np.sqrt(C)
        W_r = jax.random.uniform(ks[1], (C, C), jnp.float32, -s, s)
        W_k = jax.random.uniform(ks[2], (C, C), jnp.float32, -s, s)
        W_v = jax.random.uniform(ks[3], (C, C), jnp.float32, -s, s)
        mu_r = jax.random.uniform(ks[4], (C,), jnp.float32)
        mu_k = jax.random.uniform(ks[5], (C,), jnp.float32)
        return {'x': x, 'W_r': W_r, 'W_k': W_k, 'W_v': W_v, 'mu_r': mu_r, 'mu_k': mu_k}
    _L0_ffn_in = _L0_ffn_setup()
    _d = {'L0_attn_x': _L0_attn_in['x'], 'L0_attn_wq': _L0_attn_in['wq'], 'L0_attn_bq': _L0_attn_in['bq'], 'L0_attn_wk': _L0_attn_in['wk'], 'L0_attn_bk': _L0_attn_in['bk'], 'L0_attn_wv': _L0_attn_in['wv'], 'L0_attn_bv': _L0_attn_in['bv'], 'L0_attn_wo': _L0_attn_in['wo'], 'L0_attn_bo': _L0_attn_in['bo'], 'L0_ffn_W_r': _L0_ffn_in['W_r'], 'L0_ffn_W_k': _L0_ffn_in['W_k'], 'L0_ffn_W_v': _L0_ffn_in['W_v'], 'L0_ffn_mu_r': _L0_ffn_in['mu_r'], 'L0_ffn_mu_k': _L0_ffn_in['mu_k']}
    _x0 = _d['L0_attn_x']
    _d['L0_attn_x'] = jax.random.normal(jax.random.fold_in(jax.random.key(seed), 1), (4, 2048, 256), dtype=_x0.dtype)
    del _x0
    return _d

def reference(L0_attn_x, L0_attn_wq, L0_attn_bq, L0_attn_wk, L0_attn_bk, L0_attn_wv, L0_attn_bv, L0_attn_wo, L0_attn_bo, L0_ffn_W_r, L0_ffn_W_k, L0_ffn_W_v, L0_ffn_mu_r, L0_ffn_mu_k):

    def _L0_attn_ref(x, wq, bq, wk, bk, wv, bv, wo, bo):
        import jax, jax.numpy as jnp
        import numpy as np
        NUM_HEADS = 16
        ATT_WINDOW = 128
        GLOBAL_SIZE = 64
        B, S, HID = x.shape
        H = NUM_HEADS
        D = HID // H
        W = ATT_WINDOW
        G = GLOBAL_SIZE
        scale = D ** (-0.5)
        q = (x @ wq.T + bq).reshape(B, S, H, D)
        k = (x @ wk.T + bk).reshape(B, S, H, D)
        v = (x @ wv.T + bv).reshape(B, S, H, D)
        nW = S // W
        qw = q.reshape(B, nW, W, H, D)
        kw = k.reshape(B, nW, W, H, D)
        loc = jnp.einsum('bnihd,bnjhd->bnihj', qw, kw) * scale
        scores = jnp.zeros((B, nW, W, H, nW, W), x.dtype)
        n_idx = jnp.arange(nW)
        scores = scores.at[:, n_idx, :, :, n_idx, :].set(loc.transpose(1, 0, 2, 3, 4))
        scores = scores.reshape(B, S, H, S)
        gi = jnp.arange(0, S, S // G)
        gq = q[:, gi]
        gk = k[:, gi]
        gsc = jnp.einsum('bihd,bjhd->bihj', gq, gk) * scale
        scores = scores.at[:, gi[:, None], :, gi[None, :]].add(gsc.transpose(1, 3, 0, 2))
        attn = jax.nn.softmax(scores, axis=-1)
        out = jnp.einsum('bihj,bjhd->bihd', attn, v).reshape(B, S, HID)
        return out @ wo.T + bo

    def _L0_ffn_ref(x, W_r, W_k, W_v, mu_r, mu_k):
        import jax, jax.numpy as jnp
        import numpy as np
        DIM = 256

        def _reference_tuple_inner(x, W_r, W_k, W_v, mu_r, mu_k):
            B, T, C = x.shape
            x_prev = jnp.concatenate([jnp.zeros((B, 1, C), x.dtype), x[:, :-1, :]], axis=1)
            xr = mu_r * x + (1.0 - mu_r) * x_prev
            xk = mu_k * x + (1.0 - mu_k) * x_prev
            r = jax.nn.sigmoid(jnp.einsum('btc,dc->btd', xr, W_r))
            k = jnp.einsum('btc,dc->btd', xk, W_k)
            k_act = jnp.square(jax.nn.relu(k))
            out = r * jnp.einsum('btc,dc->btd', k_act, W_v)
            new_state = x[:, -1, :]
            return (out, new_state)
        return _reference_tuple_inner(x, W_r, W_k, W_v, mu_r, mu_k)[0]
    x = L0_attn_x
    x = _layernorm(x + _L0_attn_ref(x, L0_attn_wq, L0_attn_bq, L0_attn_wk, L0_attn_bk, L0_attn_wv, L0_attn_bv, L0_attn_wo, L0_attn_bo), axis=-1)
    x = _layernorm(x + _L0_ffn_ref(x, L0_ffn_W_r, L0_ffn_W_k, L0_ffn_W_v, L0_ffn_mu_r, L0_ffn_mu_k), axis=-1)
    return x

_drawn_inputs = setup_inputs


def setup_inputs(seed=0):
    import zlib

    import numpy as np

    out = dict(_drawn_inputs(seed))
    spreads = {}
    factors = {'L0_attn_wq': 8.0,
     'L0_attn_bq': 8.0,
     'L0_attn_wk': 8.0,
     'L0_attn_bk': 52.837,
     'L0_attn_wv': 8.0,
     'L0_attn_bv': 8.0,
     'L0_attn_wo': 8.0,
     'L0_attn_bo': 15.236,
     'L0_ffn_W_r': 3.181,
     'L0_ffn_mu_r': 6.402}
    for name, (base, spread) in spreads.items():
        noise = np.random.default_rng([zlib.crc32(name.encode()), seed]).standard_normal(out[name].shape)
        drawn = base * np.exp(spread * noise) if base else spread * noise
        out[name] = jnp.asarray(drawn.astype(out[name].dtype))
    for name, factor in factors.items():
        out[name] = (out[name] * factor).astype(out[name].dtype)
    return out
```

```python
import concourse.bass as bass
from concourse import mybir
from contextlib import ExitStack

BATCH, SEQ, HID, HEADS = 4, 2048, 256, 16
HEAD = HID // HEADS
WIN = 128
GLOB = 64
GAP = SEQ // GLOB
GPW = WIN // GAP
CW = 4
CT = CW * WIN
CHUNKS = BATCH * SEQ // CT
CPB = SEQ // CT
KC = HID // 128
GH = 4
NG = HEADS // GH
VW = HEAD + 1
NV = HEADS * VW
COR = NV + HEADS
QPART = [0, 0, 0, 1, 1, 2]
KPART = [0, 1, 2, 0, 1, 0]
NPROD = len(QPART)
SROWS = NPROD * HEAD
SCALE = HEAD ** -0.5
EPS = 1e-5


class Chunk:

    def __init__(self, i, c):
        self.i, self.c = i, c
        self.p = c % 2

    def shift(self, d):
        return Chunk(self.i, self.c + d)

    def exists(self):
        return self.i is not None or 0 <= self.c < CHUNKS

    def is_first(self):
        return self.i is None and self.c == 0

    def number(self):
        return self.c if self.i is None else self.i * 2 + self.c

    def count(self, per_chunk, more):
        if self.i is None:
            return self.c * per_chunk + more
        assert self.c * per_chunk + more > 0
        return self.i * (2 * per_chunk) + (self.c * per_chunk + more)

    def half_count(self, per_chunk):
        if self.i is None:
            return (self.c // 2 + 1) * per_chunk
        return self.i * per_chunk + (self.c // 2 + 1) * per_chunk


def back(ch, w, d):
    q, r = divmod(w - d, CW)
    return ch.shift(q), r


def upto(eng, sem, value):
    if isinstance(value, int) and value <= 0:
        return
    eng.wait_ge(sem, value)


LOOP_FROM, LOOP_TIMES, LAST = 3, 5, CHUNKS + 2


def walk(eng, step):
    for c in range(LOOP_FROM):
        for w in range(CW):
            step(Chunk(None, c), w)
    with eng.Fori(0, LOOP_TIMES) as i:
        for c in range(LOOP_FROM, LOOP_FROM + 2):
            for w in range(CW):
                step(Chunk(i, c), w)
    for c in range(LOOP_FROM + 2 * LOOP_TIMES, LAST):
        for w in range(CW):
            step(Chunk(None, c), w)


def build(nc, x, xT, xgT, wq, wk, wv, wo, wr, wk2, wv2, bqk, bv, bo, mu_rk, out):
    f32, bf16 = mybir.dt.float32, mybir.dt.bfloat16
    ALU, ACT, AX = mybir.AluOpType, mybir.ActivationFunctionType, mybir.AxisListType

    x_tok = x.rearrange("(n w p) f -> n p w f", w=CW, p=WIN)
    out_tok = out.rearrange("(n w p) f -> n p w f", w=CW, p=WIN)
    xT_v = xT.rearrange("(k p) (n t) -> n p k t", p=128, t=CT)
    xT_b = xT.rearrange("(k p) (b t) -> b p k t", p=128, b=BATCH)
    parts_dram = nc.dram_tensor("parts_dram", (2, 2, KC, 3, 128, CT), bf16, kind="Internal").ap()
    cor_dram = nc.dram_tensor("cor_dram", (BATCH * GLOB, COR), f32, kind="Internal").ap()
    vsum_dram = nc.dram_tensor("vsum_dram", (CHUNKS, NV), f32, kind="Internal").ap()
    cor_v = cor_dram.rearrange("(n w r) f -> n r w f", w=CW, r=GPW)
    vsum_v = vsum_dram.rearrange("(b c) f -> c b f", c=CPB)

    ctx = ExitStack()
    with ctx:
        def sb(name, shape, dt=f32):
            return ctx.enter_context(nc.sbuf_tensor(name, shape, dt))

        def pb(name, shape):
            return ctx.enter_context(nc.psum_tensor(name, shape, f32))

        def sem(name):
            return ctx.enter_context(nc.semaphore(name))

        W = {k: sb("w_" + k, [128, KC, HID]) for k in ("q", "k", "v", "o", "r", "k2", "v2")}
        W_DRAM = dict(q=wq, k=wk, v=wv, o=wo, r=wr, k2=wk2, v2=wv2)
        b_col = sb("b_col", [128, 2, KC])
        bv_row = sb("bv_row", [128, HID])
        bo_row = sb("bo_row", [128, HID])
        mu = sb("mu", [128, 2, KC])
        one_mu = sb("one_mu", [128, 2, KC])
        keep = sb("keep", [128, CHUNKS])
        ident = sb("ident", [128, 128])
        ident_h = sb("ident_h", [128, 128], bf16)
        ones = sb("ones", [128, 128])
        sel = sb("sel", [3 * HEADS, HEADS], bf16)
        minus_half = sb("minus_half", [128, 1])
        eps = sb("eps", [128, 1])
        xT_sb = sb("xT_sb", [128, 2, KC, CT])
        x_sb = sb("x_sb", [128, CW, HID])
        cor = sb("cor", [128, 2, CW, COR])
        vsum = sb("vsum", [128, 2, NV])
        parts = sb("parts", [128, 2, 3, CT], bf16)
        rest = sb("rest", [128, 2, CT])
        stack = [[sb(f"stack{p}{k}", [128, HEADS, CT], bf16) for k in "qk"] for p in range(2)]
        va_all = sb("va_all", [128, 2, CW, NV + 32 - VW])
        va = va_all[:, :, :, 0:NV].rearrange("p a w (h d) -> p a w h d", h=HEADS)
        smax = sb("smax", [128, 2, HEADS])
        negm = sb("negm", [128, 2, HEADS])
        m_rest = sb("m_rest", [128, 2, HEADS])
        m_diff = sb("m_diff", [128, 2, HEADS])
        m_parts = sb("m_parts", [128, 2, 8, HEADS], bf16)
        mT = sb("mT", [3 * HEADS, 2, 128], bf16)
        e_zero = sb("e_zero", [128, 2, HEADS])
        e_cor = sb("e_cor", [128, 2, HEADS])
        pT = sb("pT", [128, 2, HEADS, WIN])
        av = sb("av", [128, 2, NG * WIN])
        vwin = sb("vwin", [128, 2, NV])
        t_rest = sb("t_rest", [128, NV])
        t_cor = sb("t_cor", [128, NV])
        other = sb("other", [128, 2, NV])
        num = sb("num", [128, 2, HEADS, VW])
        rden = sb("rden", [128, 2, HEADS])
        att = sb("att", [128, 2, HID])
        attT = sb("attT", [128, 2, KC, WIN])
        x_bo = sb("x_bo", [128, 2, HID])
        y = sb("y", [128, 2, HID])
        st1 = sb("st1", [128, 2, 6])
        mv1 = sb("mv1", [128, 2, 2])
        ve1 = sb("ve1", [128, 2, 1])
        rs1 = sb("rs1", [128, 2, 1])
        x1 = sb("x1", [128, 8, HID])
        x1T = sb("x1T", [128, 2, KC, CT + 1])
        mix_a = sb("mix_a", [128, KC, CT])
        xk = sb("xk", [128, KC, CT])
        xr = sb("xr", [128, KC, CT])
        kact = sb("kact", [128, KC, CT])
        th = sb("th", [128, 2, HID])
        u = sb("u", [128, 2, HID])
        z = sb("z", [128, 2, HID])
        st2 = sb("st2", [128, 2, 6])
        mv2 = sb("mv2", [128, 2, 2])
        ve2 = sb("ve2", [128, 2, 1])
        rs2 = sb("rs2", [128, 2, 1])
        o_sb = sb("o_sb", [128, 2, HID])

        flat = [stack[1][k][:, :, :].rearrange("p h t -> p (h t)").bitcast(f32) for k in range(2)]
        sum_in = [flat[0][:, SEQ * k:SEQ * (k + 1)] for k in range(2)]
        xg_sb = kact[:, :, 0:HID]
        gq = kact[:, :, HID:2 * HID]
        gk = xr[:, :, 0:HID]
        k_diag = pT[:, :, :, :].rearrange("p a h t -> p (a h t)").rearrange(
            "p (g h t) -> p g h t", g=KC, h=8)
        gs2 = [flat[1][0:GLOB, GLOB * HEADS * n:GLOB * HEADS * (n + 1)] for n in range(2)]
        gs1 = [flat[1][0:GLOB, GLOB * HEADS * n:GLOB * HEADS * (n + 1)] for n in range(2, 4)]
        x1T_flat = x1T[0:GLOB, :, :, :].rearrange("p a k t -> p (a k t)")
        gc = [x1T_flat[:, GLOB * HEADS * n:GLOB * HEADS * (n + 1)] for n in range(2)]
        gcT = [a[0:GLOB, :, :].rearrange("p k t -> p (k t)") for a in (xk, mix_a)]
        gv = av[0:GLOB, :, 0:NV].rearrange("p a (h d) -> p a h d", h=HEADS)
        g_out = x_sb[0:GLOB, :, :].rearrange("p w f -> p (w f)")[:, 0:2 * COR].rearrange("p (a f) -> p a f", a=2)
        same = sb("same", [GLOB, GLOB])
        hmask = sb("hmask", [128, 8])
        xsum = sb("xsum", [128, KC, BATCH])
        vs_sb = sb("vs_sb", [BATCH, NV])

        S = pb("S", [128, 2, 512])
        T = pb("T", [128, 2, 512])
        V = pb("V", [128, 512])
        A = pb("A", [128, 512])
        B = pb("B", [128, 512])
        C = pb("C", [128, 512])

        w_in = sem("w_in")
        xg_in = sem("xg_in")
        xT_in = [sem(f"xT_in{p}") for p in range(2)]
        x_in = [sem(f"x_in{p}") for p in range(2)]
        cor_in = [sem(f"cor_in{p}") for p in range(2)]
        sum_loaded = [sem(f"sum_loaded{p}") for p in range(2)]
        parts_out = sem("parts_out")
        stack_in = [sem(f"stack_in{p}") for p in range(2)]
        scratch_out = sem("scratch_out")
        y_out = [sem(f"y_out{p}") for p in range(2)]
        const_done = sem("const_done")
        dve_const = sem("dve_const")
        one_mu_done = sem("one_mu_done")
        g_proj = sem("g_proj")
        g_qk = sem("g_qk")
        g_diag = sem("g_diag")
        g_score = sem("g_score")
        g_vp = sem("g_vp")
        g_v = sem("g_v")
        g_arg = sem("g_arg")
        g_exp = sem("g_exp")
        g_cor = sem("g_cor")
        g_tr = sem("g_tr")
        g_cT = sem("g_cT")
        g_num = sem("g_num")
        g_row = sem("g_row")
        g_stored = [sem(f"g_stored{p}") for p in range(2)]
        x_summed = sem("x_summed")
        vs_proj = sem("vs_proj")
        vs_done = sem("vs_done")
        qk_mm = sem("qk_mm")
        v_mm = sem("v_mm")
        s_mm = sem("s_mm")
        mT_mm = sem("mT_mm")
        t_mm = sem("t_mm")
        pv_mm = sem("pv_mm")
        vwin_mm = sem("vwin_mm")
        avT_mm = sem("avT_mm")
        attT_mm = sem("attT_mm")
        wo_mm = sem("wo_mm")
        x1T_mm = sem("x1T_mm")
        k2_mm = sem("k2_mm")
        r_mm = sem("r_mm")
        v2_mm = sem("v2_mm")
        part1 = sem("part1")
        part2 = sem("part2")
        relu_done = sem("relu_done")
        kact_done = sem("kact_done")
        mix_a_done = sem("mix_a_done")
        mT_sb = sem("mT_sb")
        exp_done = sem("exp_done")
        av_sb = sem("av_sb")
        vwin_sb = sem("vwin_sb")
        e_done = sem("e_done")
        attT_sb = sem("attT_sb")
        x1T_sb = sem("x1T_sb")
        th_done = sem("th_done")
        rest_done = sem("rest_done")
        va_done = sem("va_done")
        smax_done = sem("smax_done")
        negm_done = sem("negm_done")
        att_done = sem("att_done")
        mv1_done = sem("mv1_done")
        x1_done = sem("x1_done")
        halo_done = sem("halo_done")
        mix_done = sem("mix_done")
        v2_used = sem("v2_used")
        mv2_done = sem("mv2_done")
        o_done = sem("o_done")
        dve_seq = sem("dve_seq")
        parts_done = sem("parts_done")
        m_diff_done = sem("m_diff_done")
        m_parts_done = sem("m_parts_done")
        other_done = sem("other_done")
        x_bo_done = sem("x_bo_done")
        rs1_done = sem("rs1_done")
        rs2_done = sem("rs2_done")
        pool_seq = sem("pool_seq")

        class Chain:

            def __init__(self, eng, semaphore):
                self.eng, self.sem, self.n = eng, semaphore, 0

            def link(self, ins):
                self.n += 1
                ins.then_inc(self.sem, 1)

            def after(self):
                self.eng.wait_ge(self.sem, self.n)

            def restart(self):
                if self.n:
                    self.after()
                    self.eng.sem_clear(self.sem)
                    self.n = 0

        N_FIRST, N_REST = 6, 6
        block = ctx.enter_context(nc.Block())

        @block.sync
        def _(sp):
            sp.dma_start(xg_sb, xgT.rearrange("(k p) t -> p k t", p=128)).then_inc(xg_in, 16)
            for k in ("q", "k", "v"):
                sp.dma_start(W[k][:, :, :], W_DRAM[k].rearrange("(k p) n -> p k n", p=128)).then_inc(xg_in, 16)
            sp.dma_start(b_col[:, :, :], bqk).then_inc(xg_in, 16)
            sp.dma_start(bv_row[:, :], bv.partition_broadcast(128)).then_inc(xg_in, 16)

            def load_xT(ch):
                if not ch.exists():
                    return
                upto(sp, v_mm, ch.count(CW, -CW))
                sp.dma_start(xT_sb[:, ch.p, :, :], xT_v[bass.ds(ch.number(), 1)].rearrange("o p k t -> p (o k) t")
                             ).then_inc(xT_in[ch.p], 16)

            def load_tokens(ch):
                if not ch.exists():
                    return
                upto(sp, other_done, ch.count(CW, -CW))
                n = bass.ds(ch.number(), 1)
                sp.dma_start(cor[0:WIN:GAP, ch.p, :, :], cor_v[n].rearrange("o r w f -> r (o w) f")
                             ).then_inc(cor_in[ch.p], 16)
                sp.dma_start(vsum[:, ch.p, :], vsum_dram[n].rearrange("o f -> (o f)").partition_broadcast(128)
                             ).then_inc(cor_in[ch.p], 16)

            def load_x(ch, half):
                upto(sp, x_bo_done, ch.count(CW, -CW + 2 * (half + 1)))
                sp.dma_start(x_sb[:, 2 * half:2 * half + 2, :],
                             x_tok[bass.ds(ch.number(), 1)].rearrange("o p w f -> p (o w) f")[:, 2 * half:2 * half + 2, :]
                             ).then_inc(x_in[half], 16)

            load_xT(Chunk(None, 0))
            for k in range(2):
                sp.dma_start(sum_in[k], xT_b[0, :, k, :]).then_inc(sum_loaded[k], 16)
            for k in ("o", "r", "k2", "v2"):
                sp.dma_start(W[k][:, :, :], W_DRAM[k].rearrange("(k p) n -> p k n", p=128)).then_inc(w_in, 16)
            sp.dma_start(mu[:, :, :], mu_rk).then_inc(w_in, 16)
            sp.dma_start(bo_row[:, :], bo.partition_broadcast(128)).then_inc(w_in, 16)

            def now(value):
                return value if isinstance(value, int) else sp.snap(sp.to_reg(value))

            def restack(m, un):
                kind, g = un % 2, un // 2
                if un == 0:
                    read_at = now(m.count(CW * NG, -CW * NG))
                split_at = now(m.count(4, un + 1))
                stored_at = now(m.count(4 * 16, 16 * (un + 1)))
                if un == 0:
                    upto(sp, t_mm, read_at)
                sp.wait_ge(parts_done, split_at)
                sp.dma_start(parts_dram[m.p, kind, g].rearrange("s p t -> p s t"), parts[:, un % 2, :, :]
                             ).then_inc(parts_out, 16)
                sp.wait_ge(parts_out, stored_at)
                for pr, s in enumerate(KPART if kind else QPART):
                    sp.dma_start(stack[m.p][kind][HEAD * pr:HEAD * (pr + 1), 8 * g:8 * g + 8, :],
                                 parts_dram[m.p, kind, g, s].rearrange("(h d) t -> d h t", d=HEAD)
                                 ).then_inc(stack_in[m.p], 16)

            for un in range(4):
                restack(Chunk(None, 0), un)
            for b in range(BATCH):
                if b + 1 < BATCH:
                    for k in range(KC):
                        sp.wait_ge(x_summed, KC * b + k + 1)
                        sp.dma_start(sum_in[k], xT_b[b + 1, :, k, :]).then_inc(sum_loaded[k], 16)
                sp.wait_ge(g_row, b + 1)
                sp.dma_start(cor_dram[b * GLOB:(b + 1) * GLOB, :], g_out[:, b % 2, :]).then_inc(g_stored[b % 2], 16)
            sp.wait_ge(vs_done, 1)
            for c in range(CPB):
                sp.dma_start(vsum_v[c], vs_sb[:, :]).then_inc(scratch_out, 16)
            for p in range(2):
                sp.wait_ge(g_stored[p], 16 * BATCH // 2)
            sp.wait_ge(scratch_out, 16 * CPB)
            load_tokens(Chunk(None, 0))
            load_xT(Chunk(None, 1))

            def store(f, fw):
                if f.exists():
                    sp.wait_ge(o_done, f.count(CW, fw + 1))
                    n = bass.ds(f.number(), 1)
                    sp.dma_start(out_tok[n].rearrange("o p w f -> p (o w) f")[:, fw, :], o_sb[:, fw % 2, :]
                                 ).then_inc(y_out[fw % 2], 16)

            def step(ch, w):
                nxt = ch.shift(1)
                if w == 0:
                    load_xT(ch.shift(2))
                if w % 2 == 0 and ch.exists():
                    load_x(ch, w // 2)
                if w == 2:
                    load_tokens(nxt)
                if w < 2 and nxt.exists():
                    restack(nxt, 2 * w)
                    restack(nxt, 2 * w + 1)
                store(*back(ch, w, 8))

            walk(sp, step)
            for p in range(2):
                sp.wait_ge(y_out[p], 16 * CHUNKS * CW // 2)

        @block.tensor
        def _(pe):
            mm, tr = nc.tensor.matmul, nc.tensor.transpose

            def project(dst, lhs, rhs):
                for kc in range(KC):
                    last = mm(dst, lhs(kc), rhs(kc), start=(kc == 0), stop=(kc == KC - 1))
                return last

            pe.wait_ge(xg_in, 16 * N_FIRST)
            banks = [S[:, 0], S[:, 1], T[:, 0], T[:, 1]]
            for n, (k, g) in enumerate((k, g) for k in "qk" for g in range(KC)):
                project(banks[n][:, 0:HID], lambda kc: W[k][:, kc, 128 * g:128 * g + 128],
                        lambda kc: xg_sb[:, kc, :]).then_inc(g_proj, 1)

            def unit(m, un):
                kind, g = un % 2, un // 2
                if un == 0:
                    pe.wait_ge(xT_in[m.p], m.half_count(16))
                    upto(pe, va_done, m.count(CW, 0))
                else:
                    pe.wait_ge(rest_done, m.count(4, un))
                project(A[:, :], lambda kc: W["qk"[kind]][:, kc, 128 * g:128 * g + 128],
                        lambda kc: xT_sb[:, m.p, kc, :]).then_inc(qk_mm, 1)

            def v_unit(m, w):
                project(A[:, 0:HID], lambda kc: xT_sb[:, m.p, kc, WIN * w:WIN * (w + 1)],
                        lambda kc: W["v"][:, kc, :]).then_inc(v_mm, 1)

            first = Chunk(None, 0)
            for un in range(4):
                unit(first, un)
            pe.wait_ge(rest_done, 4)
            for w in range(CW):
                if w:
                    pe.wait_ge(va_done, w)
                v_unit(first, w)

            pe.wait_ge(const_done, 1)
            for b in range(BATCH):
                tok = slice(GLOB * b, GLOB * (b + 1))
                if b == 0:
                    pe.wait_ge(g_diag, KC)
                    pe.wait_ge(g_qk, 4)
                else:
                    pe.wait_ge(g_arg, b)
                for g in range(KC):
                    last = mm(S[0:GLOB, g, :], gq[:, g, tok], k_diag[:, g, :, tok], start=True, stop=True)
                last.then_inc(g_score, 1)
                if b:
                    pe.wait_ge(g_v, b)
                project(V[0:GLOB, 0:HID], lambda kc: xg_sb[:, kc, tok], lambda kc: W["v"][:, kc, :]
                        ).then_inc(g_vp, 1)
                pe.wait_ge(g_cor, b + 1)
                for h in range(HEADS):
                    last = tr(T[0:GLOB, h // 8, GLOB * (h % 8):GLOB * (h % 8 + 1)],
                              gc[b % 2][:, GLOB * h:GLOB * (h + 1)], ident[0:GLOB, 0:GLOB])
                last.then_inc(g_tr, 1)
                pe.wait_ge(g_cT, b + 1)
                pe.wait_ge(g_v, b + 1)
                if b:
                    pe.wait_ge(g_row, b)
                for h in range(HEADS):
                    last = mm(B[0:GLOB, VW * h:VW * (h + 1)], gcT[b % 2][:, GLOB * h:GLOB * (h + 1)],
                              gv[:, b % 2, h, :], start=True, stop=True)
                last.then_inc(g_num, 1)
            pe.wait_ge(x_summed, KC * BATCH)
            project(V[0:BATCH, 0:HID], lambda kc: xsum[:, kc, :], lambda kc: W["v"][:, kc, :]).then_inc(vs_proj, 1)

            def scores(ch, w, g):
                if w == 0 and g == 0:
                    pe.wait_ge(stack_in[ch.p], ch.half_count(16 * 4 * NPROD))
                upto(pe, smax_done, ch.count(CW * NG, NG * w + g - 1))
                q, k = stack[ch.p]
                tok = slice(WIN * w, WIN * (w + 1))
                for j in range(GH):
                    h = GH * g + j
                    last = mm(S[:, g % 2, WIN * j:WIN * (j + 1)], q[0:SROWS, h, tok], k[0:SROWS, h, tok],
                              start=True, stop=True)
                last.then_inc(s_mm, 1)

            def scores_T(ch, w, g):
                if g == 0:
                    pe.wait_ge(mT_sb, ch.count(CW, w + 1))
                upto(pe, exp_done, ch.count(CW * NG, NG * w + g - 1))
                q, k = stack[ch.p]
                tok = slice(WIN * w, WIN * (w + 1))
                for j in range(GH):
                    h = GH * g + j
                    dst = T[:, g % 2, WIN * j:WIN * (j + 1)]
                    mm(dst, k[0:SROWS, h, tok], q[0:SROWS, h, tok], start=True, stop=False)
                    last = mm(dst, sel[:, h:h + 1].broadcast_to([3 * HEADS, WIN]), mT[:, w % 2, :], start=False, stop=True)
                last.then_inc(t_mm, 1)

            def times_v(ch, w, g):
                pe.wait_ge(exp_done, ch.count(CW * NG, NG * w + g + 1))
                if g == 0:
                    upto(pe, av_sb, ch.count(CW, w))
                for j in range(GH):
                    h = GH * g + j
                    last = mm(V[32 * j:32 * (j + 1), WIN * g:WIN * (g + 1)], va_all[:, ch.p, w, VW * h:VW * h + 32],
                              pT[:, w % 2, h, :], start=True, stop=True)
                if g == NG - 1:
                    last.then_inc(pv_mm, 1)

            def step(ch, w):
                nxt, prev = ch.shift(1), ch.shift(-1)
                s, t = ch.exists(), back(ch, w, 1)
                o, l = back(ch, w, 2), back(ch, w, 3)
                f = back(ch, w, 7)
                f_before = back(ch, w, 8)

                if s:
                    scores(ch, w, 0)
                    scores(ch, w, 1)
                if nxt.exists():
                    if w < 2:
                        unit(nxt, 2 * w)
                    elif w == 2:
                        pe.wait_ge(rest_done, nxt.count(4, 4))
                        v_unit(nxt, 0)
                if l[0].exists():
                    pe.wait_ge(x1_done, l[0].count(CW, l[1] + 1))
                    for kc in range(KC):
                        last = tr(B[:, 128 * kc:128 * (kc + 1)],
                                  x1[:, 4 * l[0].p + l[1], 128 * kc:128 * (kc + 1)], ident[:, :])
                    last.then_inc(x1T_mm, 1)
                if t[0].exists():
                    if f_before[0].exists():
                        pe.wait_ge(v2_used, f_before[0].count(CW, f_before[1] + 1))
                    else:
                        upto(pe, vwin_sb, t[0].count(CW, t[1]))
                    pe.wait_ge(m_parts_done, t[0].count(CW, t[1] + 1))
                    tr(C[:, 0:64].bitcast(bf16), m_parts[:, t[1] % 2, :, :].rearrange("p s h -> p (s h)"),
                       ident_h[:, :]).then_inc(mT_mm, 1)
                if s:
                    scores(ch, w, 2)
                if o[0].exists():
                    upto(pe, x1T_sb, o[0].count(CW, o[1]))
                    pe.wait_ge(av_sb, o[0].count(CW, o[1] + 1))
                    for g in range(NG):
                        last = tr(B[:, 128 * g:128 * (g + 1)], av[:, o[1] % 2, WIN * g:WIN * (g + 1)], ident[:, :])
                    last.then_inc(avT_mm, 1)
                if s:
                    scores(ch, w, 3)
                if w == 3 and prev.exists():
                    pe.wait_ge(relu_done, prev.count(KC, 1))
                    project(A[:, :], lambda kc: W["k2"][:, kc, 128:256], lambda kc: xk[:, kc, :]).then_inc(k2_mm, 1)
                if t[0].exists():
                    scores_T(*t, 0)
                    scores_T(*t, 1)
                    mm(C[:, 0:NV], ones[:, :], va[:, t[0].p, t[1], :, 0:VW], start=True, stop=True
                       ).then_inc(vwin_mm, 1)
                if nxt.exists():
                    if w < 2:
                        unit(nxt, 2 * w + 1)
                    elif w == 2:
                        pe.wait_ge(va_done, nxt.count(CW, 1))
                        v_unit(nxt, 1)
                    else:
                        if prev.exists():
                            pe.wait_ge(relu_done, prev.count(KC, 2))
                        else:
                            pe.wait_ge(va_done, nxt.count(CW, 2))
                        v_unit(nxt, 2)
                if o[0].exists():
                    pe.wait_ge(att_done, o[0].count(CW, o[1] + 1))
                    for kc in range(KC):
                        last = tr(B[:, 128 * kc:128 * (kc + 1)], att[:, o[1] % 2, 128 * kc:128 * (kc + 1)],
                                  ident[:, :])
                    last.then_inc(attT_mm, 1)
                if t[0].exists():
                    scores_T(*t, 2)
                    scores_T(*t, 3)
                if f[0].exists():
                    if t[0].exists():
                        pe.wait_ge(vwin_sb, t[0].count(CW, t[1] + 1))
                    else:
                        pe.wait_ge(v2_used, f_before[0].count(CW, f_before[1] + 1))
                    pe.wait_ge(mix_done, f[0].count(2, 2))
                    project(C[:, 0:HID], lambda kc: xr[:, kc, WIN * f[1]:WIN * (f[1] + 1)],
                            lambda kc: W["r"][:, kc, :]).then_inc(r_mm, 1)
                if t[0].exists():
                    times_v(*t, 0)
                    times_v(*t, 1)
                if o[0].exists():
                    pe.wait_ge(attT_sb, o[0].count(CW, o[1] + 1))
                    project(B[:, 0:HID], lambda kc: attT[:, o[1] % 2, kc, :], lambda kc: W["o"][:, kc, :]
                            ).then_inc(wo_mm, 1)
                if t[0].exists():
                    times_v(*t, 2)
                    times_v(*t, 3)
                if nxt.exists() and w == 3:
                    pe.wait_ge(va_done, nxt.count(CW, 3))
                    v_unit(nxt, 3)
                if w == 2 and prev.exists():
                    if nxt.exists():
                        pe.wait_ge(va_done, nxt.count(CW, 2))
                    else:
                        upto(pe, relu_done, prev.count(KC, 0))
                    pe.wait_ge(mix_done, prev.count(2, 1))
                    project(A[:, :], lambda kc: W["k2"][:, kc, 0:128], lambda kc: xk[:, kc, :]).then_inc(k2_mm, 1)
                if f[0].exists():
                    pe.wait_ge(th_done, f[0].count(CW, f[1] + 1))
                    pe.wait_ge(kact_done, f[0].count(KC, KC))
                    project(C[:, 0:HID], lambda kc: kact[:, kc, WIN * f[1]:WIN * (f[1] + 1)],
                            lambda kc: W["v2"][:, kc, :]).then_inc(v2_mm, 1)

            pe.wait_ge(const_done, 2)
            pe.wait_ge(w_in, 16 * N_REST)
            walk(pe, step)

        @block.scalar
        def _(act):
            fn = nc.scalar.activation
            act.wait_ge(xg_in, 16 * N_FIRST)
            banks = [S[:, 0], S[:, 1], T[:, 0], T[:, 1]]
            for n in range(4):
                kind, g = n // 2, n % 2
                act.wait_ge(g_proj, n + 1)
                fn((gk if kind else gq)[:, g, :], banks[n][:, 0:HID], ACT.Identity,
                   bias=b_col[:, kind, g:g + 1]).then_inc(g_qk, 1)

            def first_part(m, un):
                kind, g = un % 2, un // 2
                act.wait_ge(qk_mm, m.count(4, un + 1))
                upto(act, parts_out, m.count(64, 16 * (un - 1)))
                fn(parts[:, un % 2, 0, :], A[:, :], ACT.Identity, bias=b_col[:, kind, g:g + 1]).then_inc(part1, 1)

            def second_part(m, un):
                act.wait_ge(rest_done, m.count(4, un + 1))
                fn(parts[:, un % 2, 1, :], rest[:, un % 2, :], ACT.Identity).then_inc(part2, 1)

            for un in range(4):
                first_part(Chunk(None, 0), un)
                second_part(Chunk(None, 0), un)

            def sum_x(b):
                for kc in range(KC):
                    act.wait_ge(sum_loaded[kc], 16 * (b + 1))
                    fn(sum_in[kc], sum_in[kc], ACT.Identity,
                       accum_out=xsum[:, kc, b:b + 1]).then_inc(x_summed, 1)

            for b in range(BATCH):
                act.wait_ge(g_arg, b + 1)
                fn(gs2[b % 2], gs2[b % 2], ACT.Exp, scale=SCALE)
                fn(gs1[b % 2], gs1[b % 2], ACT.Exp, scale=SCALE).then_inc(g_exp, 1)
                sum_x(b)
                act.wait_ge(g_tr, b + 1)
                fn(gcT[b % 2], T[0:GLOB, :, :].rearrange("p a t -> p (a t)"), ACT.Copy).then_inc(g_cT, 1)

            def share_of_before(ch, which):
                for kc in range(KC):
                    fn(mix_a[:, kc, :], x1T[:, ch.p, kc, 0:CT], ACT.Identity,
                       scale=one_mu[:, which, kc:kc + 1]).then_inc(mix_a_done, 1)

            def relu(ch, half):
                act.wait_ge(k2_mm, ch.count(KC, half + 1))
                upto(act, v2_mm, ch.count(CW, 0))
                fn(kact[:, half, :], A[:, :], ACT.Relu).then_inc(relu_done, 1)

            def square(ch, half):
                act.wait_ge(relu_done, ch.count(KC, half + 1))
                fn(kact[:, half, :], kact[:, half, :], ACT.Square).then_inc(kact_done, 1)

            act.wait_ge(one_mu_done, 1)

            def step(ch, w):
                nxt, prev = ch.shift(1), ch.shift(-1)
                s, t = ch.exists(), back(ch, w, 1)
                o, l = back(ch, w, 2), back(ch, w, 3)
                f = back(ch, w, 7)
                if nxt.exists() and w < 2:
                    first_part(nxt, 2 * w)
                if l[0].exists():
                    act.wait_ge(x1T_mm, l[0].count(CW, l[1] + 1))
                    if l[1] == 0:
                        upto(act, mix_done, l[0].count(2, -2))
                    fn(x1T[:, l[0].p, :, 1 + WIN * l[1]:1 + WIN * (l[1] + 1)],
                       B[:, 0:HID].rearrange("p (k t) -> p k t", k=KC), ACT.Copy).then_inc(x1T_sb, 1)
                if t[0].exists():
                    act.wait_ge(mT_mm, t[0].count(CW, t[1] + 1))
                    fn(mT[:, t[1] % 2, :], C[0:3 * HEADS, 0:64].bitcast(bf16), ACT.Copy).then_inc(mT_sb, 1)

                if w == 3 and prev.exists():
                    square(prev, 0)
                    relu(prev, 1)

                def exps(g):
                    act.wait_ge(t_mm, t[0].count(CW * NG, NG * t[1] + g + 1))
                    if g == 0:
                        upto(act, pv_mm, t[0].count(CW, t[1] - 1))
                    fn(pT[:, t[1] % 2, GH * g:GH * (g + 1), :], T[:, g % 2, :].rearrange("p (h q) -> p h q", h=GH),
                       ACT.Exp, scale=SCALE).then_inc(exp_done, 1)

                if t[0].exists():
                    exps(0)
                    exps(1)
                    act.wait_ge(vwin_mm, t[0].count(CW, t[1] + 1))
                    upto(act, other_done, t[0].count(CW, t[1] - 1))
                    fn(vwin[:, t[1] % 2, :], C[:, 0:NV], ACT.Copy).then_inc(vwin_sb, 1)
                if w == 3 and prev.exists():
                    square(prev, 1)
                if w == 2 and prev.exists():
                    act.wait_ge(halo_done, prev.count(1, 1))
                    upto(act, mix_done, prev.count(2, 0))
                    share_of_before(prev, 1)
                if nxt.exists() and w < 2:
                    second_part(nxt, 2 * w)
                    first_part(nxt, 2 * w + 1)
                if o[0].exists():
                    act.wait_ge(attT_mm, o[0].count(CW, o[1] + 1))
                    fn(attT[:, o[1] % 2, :, :], B[:, 0:HID].rearrange("p (k t) -> p k t", k=KC), ACT.Copy
                       ).then_inc(attT_sb, 1)
                if t[0].exists():
                    exps(2)
                    exps(3)
                if nxt.exists() and w < 2:
                    second_part(nxt, 2 * w + 1)
                if f[0].exists():
                    act.wait_ge(r_mm, f[0].count(CW, f[1] + 1))
                    upto(act, v2_used, f[0].count(CW, f[1] - 1))
                    fn(th[:, f[1] % 2, :], C[:, 0:HID], ACT.Tanh, scale=0.5).then_inc(th_done, 1)
                if t[0].exists():
                    act.wait_ge(pv_mm, t[0].count(CW, t[1] + 1))
                    upto(act, avT_mm, t[0].count(CW, t[1] - 1))
                    fn(av[:, t[1] % 2, :], V[:, :], ACT.Copy).then_inc(av_sb, 1)
                if s:
                    act.wait_ge(m_diff_done, ch.count(CW, w + 1))
                    upto(act, other_done, ch.count(CW, w - 1))
                    fn(e_zero[:, w % 2, :], negm[:, w % 2, :], ACT.Exp, scale=SCALE)
                    fn(e_cor[:, w % 2, :], m_diff[:, w % 2, :], ACT.Exp, scale=SCALE).then_inc(e_done, 1)
                if w == 2 and prev.exists():
                    act.wait_ge(mix_done, prev.count(2, 1))
                    share_of_before(prev, 0)
                    relu(prev, 0)

            walk(act, step)

        @block.vector
        def _(dve):
            v = nc.vector
            chain = Chain(dve, dve_seq)
            v.memset(va_all[:, :, :, :], 1.0).then_inc(dve_const, 1)
            v.memset(cor[:, :, :, :], 0.0).then_inc(dve_const, 1)
            v.memset(gv[:, :, :, :], 1.0).then_inc(dve_const, 1)
            v.memset(vs_sb[:, :], float(SEQ)).then_inc(dve_const, 1)
            v.memset(keep[:, :], 1.0).then_inc(dve_const, 1)
            dve.wait_ge(dve_const, 5)
            v.memset(keep[:, 0:CHUNKS:CPB], 0.0).then_inc(dve_const, 1)
            dve.wait_ge(dve_const, 6)
            dve.wait_ge(const_done, 1)
            for g in range(KC):
                dve.wait_ge(g_qk, 2 + g + 1)
                v.tensor_tensor(k_diag[:, g, :, :], gk[:, g, :].unsqueeze(1).broadcast_to([128, 8, HID]),
                                hmask[:, :].unsqueeze(2).broadcast_to([128, 8, HID]), ALU.mult).then_inc(g_diag, 1)

            def rest_of(m, un):
                kind, g = un % 2, un // 2
                dve.wait_ge(part1, m.count(4, un + 1))
                upto(dve, parts_done, m.count(4, un - 1))
                v.scalar_tensor_tensor(rest[:, un % 2, :], A[:, :], b_col[:, kind, g:g + 1], parts[:, un % 2, 0, :],
                                       ALU.add, ALU.subtract).then_inc(rest_done, 1)

            def v_out(m, w):
                dve.wait_ge(v_mm, m.count(CW, w + 1))
                upto(dve, pv_mm, m.count(CW, -2 * CW + w + 1))
                upto(dve, vwin_mm, m.count(CW, -2 * CW + w + 1))
                v.tensor_tensor(va[:, m.p, w, :, 0:HEAD], A[:, 0:HID].rearrange("p (h d) -> p h d", h=HEADS),
                                bv_row[:, :].rearrange("p (h d) -> p h d", h=HEADS), ALU.add).then_inc(va_done, 1)

            for un in range(4):
                rest_of(Chunk(None, 0), un)
            for w in range(CW):
                v_out(Chunk(None, 0), w)

            for b in range(BATCH):
                p = b % 2
                row = g_out[:, p, NV:COR]
                dve.wait_ge(g_score, b + 1)
                if b >= 2:
                    dve.wait_ge(g_stored[p], 16 * (b // 2))
                sc = S[0:GLOB, :, :].rearrange("p a (h t) -> p (a h) t", t=GLOB)
                s2 = gs2[p].rearrange("p (h t) -> p h t", t=GLOB)
                s1 = gs1[p].rearrange("p (h t) -> p h t", t=GLOB)
                blk = same[:, :].unsqueeze(1).broadcast_to([GLOB, HEADS, GLOB])
                chain.link(v.scalar_tensor_tensor(s2, blk, 1.0, sc, ALU.add, ALU.mult))
                chain.link(v.tensor_tensor(s1, blk, sc, ALU.mult))
                chain.after()
                chain.link(v.tensor_reduce(row, s2, AX.X, ALU.max, negate=True))
                chain.after()
                chain.link(v.tensor_scalar(row, row, 0.0, None, ALU.min))
                chain.after()
                rb = row.unsqueeze(2).broadcast_to([GLOB, HEADS, GLOB])
                v.tensor_tensor(s2, s2, rb, ALU.add)
                v.tensor_tensor(s1, s1, rb, ALU.add).then_inc(g_arg, 1)
                dve.wait_ge(g_vp, b + 1)
                v.tensor_tensor(gv[:, p, :, 0:HEAD], V[0:GLOB, 0:HID].rearrange("p (h d) -> p h d", h=HEADS),
                                bv_row[0:GLOB, :].rearrange("p (h d) -> p h d", h=HEADS), ALU.add).then_inc(g_v, 1)
                dve.wait_ge(g_exp, b + 1)
                v.tensor_tensor(gc[p], gs2[p], gs1[p], ALU.subtract).then_inc(g_cor, 1)
                dve.wait_ge(g_num, b + 1)
                v.tensor_copy(g_out[:, p, 0:NV], B[0:GLOB, 0:NV]).then_inc(g_row, 1)
            dve.wait_ge(vs_proj, 1)
            v.scalar_tensor_tensor(vs_sb[:, :].rearrange("p (h d) -> p h d", h=HEADS)[:, :, 0:HEAD],
                                   bv_row[0:BATCH, :].rearrange("p (h d) -> p h d", h=HEADS), float(SEQ),
                                   V[0:BATCH, 0:HID].rearrange("p (h d) -> p h d", h=HEADS),
                                   ALU.mult, ALU.add).then_inc(vs_done, 1)
            dve.wait_ge(w_in, 16 * N_REST)
            v.tensor_scalar(one_mu[:, :, :], mu[:, :, :], -1.0, 1.0, ALU.mult, ALU.add).then_inc(one_mu_done, 1)

            def normalise(ch, w):
                if not ch.exists():
                    return
                p = w % 2
                dve.wait_ge(rs2_done, ch.count(CW, w + 1))
                if ch.i is not None or ch.c * CW + w >= 2:
                    dve.wait_ge(y_out[p], ch.count(32, 16 * (w // 2)))
                v.tensor_scalar(o_sb[:, p, :], z[:, p, :], mv2[:, p, 0:1], rs2[:, p, :],
                                ALU.subtract, ALU.mult).then_inc(o_done, 1)

            def step(ch, w):
                if w == 0:
                    chain.restart()
                nxt, prev = ch.shift(1), ch.shift(-1)
                s = ch.exists()
                o, l = back(ch, w, 2), back(ch, w, 3)
                f, g = back(ch, w, 7), back(ch, w, 8)
                wp, op, fp, gp = w % 2, o[1] % 2, f[1] % 2, g[1] % 2

                def maximum(g):
                    dve.wait_ge(s_mm, ch.count(CW * NG, NG * w + g + 1))
                    v.tensor_reduce(smax[:, wp, GH * g:GH * (g + 1)],
                                    S[:, g % 2, :].rearrange("p (h k) -> p h k", h=GH), AX.X, ALU.max,
                                    negate=True).then_inc(smax_done, 1)

                if s:
                    maximum(0)
                if g[0].exists():
                    dve.wait_ge(v2_used, g[0].count(CW, g[1] + 1))
                    chain.link(v.scalar_tensor_tensor(z[:, gp, :], u[:, gp, :], 0.5, x1[:, 4 * g[0].p + g[1], :],
                                                      ALU.mult, ALU.add))
                if s:
                    maximum(1)
                if g[0].exists():
                    chain.after()
                    chain.link(v.bn_stats(st2[:, gp, :], z[:, gp, :]))
                if w == 2 and prev.exists():
                    dve.wait_ge(x1T_sb, prev.count(CW, CW))
                    if not prev.is_first():
                        n = prev.number()
                        k = keep[:, n:n + 1] if isinstance(n, int) else keep[:, bass.ds(n, 1)]
                        v.tensor_scalar(x1T[:, prev.p, :, 0], x1T[:, 1 - prev.p, :, CT], k, None, ALU.mult
                                        ).then_inc(halo_done, 1)
                    else:
                        v.memset(x1T[:, prev.p, :, 0:1], 0.0).then_inc(halo_done, 1)
                if g[0].exists():
                    chain.after()
                    v.bn_aggr(mv2[:, gp, :], st2[:, gp, :]).then_inc(mv2_done, 1)
                if w == 3 and prev.exists():
                    upto(dve, r_mm, prev.count(CW, 0))
                    for kc in range(KC):
                        dve.wait_ge(mix_a_done, prev.count(2 * KC, KC + kc + 1))
                        last = v.scalar_tensor_tensor(xr[:, kc, :], x1T[:, prev.p, kc, 1:CT + 1],
                                                      mu[:, 0, kc:kc + 1], mix_a[:, kc, :], ALU.mult, ALU.add)
                    last.then_inc(mix_done, 1)
                if nxt.exists():
                    if w < 2:
                        rest_of(nxt, 2 * w)
                    elif w == 2:
                        v_out(nxt, 0)
                if s:
                    maximum(2)
                    maximum(3)
                    if w == 0:
                        dve.wait_ge(cor_in[ch.p], ch.half_count(32))
                    dve.wait_ge(smax_done, ch.count(CW * NG, NG * (w + 1)))
                    upto(dve, e_done, ch.count(CW, w - 1))
                    upto(dve, m_parts_done, ch.count(CW, w - 1))
                    v.tensor_tensor(negm[:, wp, :], smax[:, wp, :], cor[:, ch.p, w, NV:COR], ALU.min
                                    ).then_inc(negm_done, 1)
                normalise(*g)
                if o[0].exists():
                    dve.wait_ge(avT_mm, o[0].count(CW, o[1] + 1))
                    dve.wait_ge(other_done, o[0].count(CW, o[1] + 1))
                    chain.link(v.tensor_tensor(num[:, op, :, :],
                                               B[:, :].rearrange("p (h d) -> p h d", h=HEADS)[:, :, 0:VW],
                                               other[:, op, :].rearrange("p (h d) -> p h d", h=HEADS), ALU.add))
                    chain.after()
                    chain.link(v.reciprocal(rden[:, op, :], num[:, op, :, HEAD]))
                    chain.after()
                    v.tensor_tensor(att[:, op, :].rearrange("p (h d) -> p h d", h=HEADS), num[:, op, :, 0:HEAD],
                                    rden[:, op, :].unsqueeze(2).broadcast_to([128, HEADS, HEAD]), ALU.mult
                                    ).then_inc(att_done, 1)
                if nxt.exists():
                    if w < 2:
                        rest_of(nxt, 2 * w + 1)
                    elif w == 2:
                        v_out(nxt, 1)
                    else:
                        v_out(nxt, 2)
                if w == 2 and prev.exists():
                    for kc in range(KC):
                        dve.wait_ge(mix_a_done, prev.count(2 * KC, kc + 1))
                        last = v.scalar_tensor_tensor(xk[:, kc, :], x1T[:, prev.p, kc, 1:CT + 1], mu[:, 1, kc:kc + 1],
                                                      mix_a[:, kc, :], ALU.mult, ALU.add)
                    last.then_inc(mix_done, 1)
                if o[0].exists():
                    dve.wait_ge(wo_mm, o[0].count(CW, o[1] + 1))
                    dve.wait_ge(x_bo_done, o[0].count(CW, o[1] + 1))
                    chain.link(v.tensor_tensor(y[:, op, :], B[:, 0:HID], x_bo[:, op, :], ALU.add))
                    chain.after()
                    chain.link(v.bn_stats(st1[:, op, :], y[:, op, :]))
                    chain.after()
                    v.bn_aggr(mv1[:, op, :], st1[:, op, :]).then_inc(mv1_done, 1)
                if nxt.exists() and w == 3:
                    v_out(nxt, 3)
                if o[0].exists():
                    dve.wait_ge(rs1_done, o[0].count(CW, o[1] + 1))
                    v.tensor_scalar(x1[:, 4 * o[0].p + o[1], :], y[:, op, :], mv1[:, op, 0:1], rs1[:, op, :],
                                    ALU.subtract, ALU.mult).then_inc(x1_done, 1)
                if f[0].exists():
                    dve.wait_ge(v2_mm, f[0].count(CW, f[1] + 1))
                    v.scalar_tensor_tensor(u[:, fp, :], th[:, fp, :], 1.0, C[:, 0:HID], ALU.add, ALU.mult
                                           ).then_inc(v2_used, 1)

            walk(dve, step)

        @block.gpsimd
        def _(pool):
            g_ = nc.gpsimd
            chain = Chain(pool, pool_seq)
            for tile, value in ((ident, 0.0), (ident_h, 0.0), (same, 1.0), (hmask, 1.0), (sel, 0.0), (m_parts, 0.0)):
                chain.link(g_.memset(tile[:], value))
            chain.after()
            for tile in (ident, ident_h):
                g_.affine_select(out=tile[:, :], in_=tile[:, :], compare_op=ALU.not_equal, fill=1.0, base=0,
                                 pattern=[[-1, 128]], channel_multiplier=1)
            s3 = same[:, :].rearrange("p (w r) -> p w r", r=GPW)
            chain.link(g_.affine_select(out=s3, in_=s3, compare_op=ALU.is_ge, fill=0.0, base=0,
                                        pattern=[[-GPW, GLOB // GPW], [0, GPW]], channel_multiplier=1))
            chain.link(g_.affine_select(out=hmask[:, :], in_=hmask[:, :], compare_op=ALU.is_ge, fill=0.0, base=0,
                                        pattern=[[-HEAD, 8]], channel_multiplier=1))
            chain.after()
            g_.affine_select(out=s3, in_=s3, compare_op=ALU.is_ge, fill=0.0, base=GPW - 1,
                             pattern=[[GPW, GLOB // GPW], [0, GPW]], channel_multiplier=-1)
            g_.affine_select(out=hmask[:, :], in_=hmask[:, :], compare_op=ALU.is_ge, fill=0.0, base=HEAD - 1,
                             pattern=[[HEAD, 8]], channel_multiplier=-1).then_inc(const_done, 1)
            for part in range(3):
                chain.link(g_.affine_select(out=sel[:, :], in_=sel[:, :], compare_op=ALU.not_equal, fill=1.0,
                                            base=-HEADS * part, pattern=[[-1, HEADS]],
                                            channel_multiplier=1))
                chain.after()
            g_.memset(minus_half[:, :], -0.5)
            g_.memset(eps[:, :], EPS)
            g_.memset(ones[:, :], 1.0).then_inc(const_done, 1)
            pool.wait_ge(const_done, 2)

            def split(m, un):
                pool.wait_ge(part2, m.count(4, un + 1))
                g_.tensor_tensor(parts[:, un % 2, 2, :], rest[:, un % 2, :], parts[:, un % 2, 1, :], ALU.subtract
                                 ).then_inc(parts_done, 1)

            for un in range(4):
                split(Chunk(None, 0), un)
            pool.wait_ge(w_in, 16 * N_REST)

            def rstd(ve, rs, mv, done):
                chain.link(g_.tensor_tensor(ve, mv, eps[:, :], ALU.add))
                chain.after()
                g_.tensor_tensor(rs, ve, minus_half[:, :], ALU.pow).then_inc(done, 1)

            def step(ch, w):
                if w == 0:
                    chain.restart()
                nxt, prev = ch.shift(1), ch.shift(-1)
                s, t = ch.exists(), back(ch, w, 1)
                o, l = back(ch, w, 2), back(ch, w, 3)
                g = back(ch, w, 8)
                wp, tp, op, gp = w % 2, t[1] % 2, o[1] % 2, g[1] % 2
                if o[0].exists():
                    if o[1] % 2 == 0:
                        pool.wait_ge(x_in[o[1] // 2], o[0].count(16, 16))
                    upto(pool, mv1_done, o[0].count(CW, o[1] - 1))
                    g_.tensor_tensor(x_bo[:, op, :], x_sb[:, o[1], :], bo_row[:, :], ALU.add
                                     ).then_inc(x_bo_done, 1)
                if g[0].exists():
                    pool.wait_ge(mv2_done, g[0].count(CW, g[1] + 1))
                    rstd(ve2[:, gp, :], rs2[:, gp, :], mv2[:, gp, 1:2], rs2_done)
                if nxt.exists() and w < 2:
                    split(nxt, 2 * w)
                if s:
                    pool.wait_ge(negm_done, ch.count(CW, w + 1))
                    upto(pool, e_done, ch.count(CW, w - 1))
                    upto(pool, mT_mm, ch.count(CW, w - 1))
                    g_.tensor_tensor(m_diff[:, wp, :], negm[:, wp, :], cor[:, ch.p, w, NV:COR], ALU.subtract
                                     ).then_inc(m_diff_done, 1)
                    chain.link(g_.tensor_copy(m_parts[:, wp, 0, :], negm[:, wp, :]))
                    chain.after()
                    chain.link(g_.tensor_tensor(m_rest[:, wp, :], negm[:, wp, :], m_parts[:, wp, 0, :], ALU.subtract))
                    chain.after()
                    chain.link(g_.tensor_copy(m_parts[:, wp, 1, :], m_rest[:, wp, :]))
                    chain.after()
                    g_.tensor_tensor(m_parts[:, wp, 2, :], m_rest[:, wp, :], m_parts[:, wp, 1, :], ALU.subtract
                                     ).then_inc(m_parts_done, 1)
                if t[0].exists():
                    pool.wait_ge(vwin_sb, t[0].count(CW, t[1] + 1))
                    pool.wait_ge(e_done, t[0].count(CW, t[1] + 1))
                    if t[1] == 0:
                        pool.wait_ge(cor_in[t[0].p], t[0].half_count(32))
                    h3 = "p (h d) -> p h d"
                    ez = e_zero[:, tp, :].unsqueeze(2).broadcast_to([128, HEADS, VW])
                    ec = e_cor[:, tp, :].unsqueeze(2).broadcast_to([128, HEADS, VW])
                    chain.link(g_.tensor_tensor(t_rest[:, :], vsum[:, t[0].p, :], vwin[:, tp, :], ALU.subtract))
                    chain.link(g_.tensor_tensor(t_cor[:, :].rearrange(h3, h=HEADS),
                                                cor[:, t[0].p, t[1], 0:NV].rearrange(h3, h=HEADS), ec, ALU.mult))
                    chain.after()
                    if nxt.exists() and w < 2:
                        split(nxt, 2 * w + 1)
                    chain.link(g_.tensor_tensor(t_rest[:, :].rearrange(h3, h=HEADS),
                                                t_rest[:, :].rearrange(h3, h=HEADS), ez, ALU.mult))
                    chain.after()
                    upto(pool, att_done, t[0].count(CW, t[1] - 1))
                    g_.tensor_tensor(other[:, tp, :], t_rest[:, :], t_cor[:, :], ALU.add).then_inc(other_done, 1)
                elif nxt.exists() and w < 2:
                    split(nxt, 2 * w + 1)
                if o[0].exists():
                    pool.wait_ge(mv1_done, o[0].count(CW, o[1] + 1))
                    rstd(ve1[:, op, :], rs1[:, op, :], mv1[:, op, 1:2], rs1_done)

            walk(pool, step)


def kernel(L0_attn_x, L0_attn_wq, L0_attn_bq, L0_attn_wk, L0_attn_bk, L0_attn_wv, L0_attn_bv, L0_attn_wo, L0_attn_bo,
           L0_ffn_W_r, L0_ffn_W_k, L0_ffn_W_v, L0_ffn_mu_r, L0_ffn_mu_k):
    import numpy as np
    import concourse.bacc as bacc
    from concourse import mybir as mb
    from concourse.bass_utils import run_bass_kernel_spmd

    x = np.ascontiguousarray(L0_attn_x).reshape(BATCH * SEQ, HID)
    t = lambda a: np.ascontiguousarray(np.asarray(a).T)
    columns = lambda a, b: np.ascontiguousarray(np.stack([np.asarray(v).reshape(KC, 128).T for v in (a, b)], 1))
    arrays = {
        "x": x, "xT": t(x), "xgT": t(x[::GAP]),
        "wq": t(L0_attn_wq), "wk": t(L0_attn_wk), "wv": t(L0_attn_wv), "wo": t(L0_attn_wo),
        "wr": t(L0_ffn_W_r), "wk2": t(L0_ffn_W_k), "wv2": t(L0_ffn_W_v),
        "bqk": columns(L0_attn_bq, L0_attn_bk), "bv": np.asarray(L0_attn_bv),
        "bo": np.asarray(L0_attn_bo), "mu_rk": columns(L0_ffn_mu_r, L0_ffn_mu_k),
    }
    nc = bacc.Bacc("TRN2", target_bir_lowering=False, num_devices=1)
    aps = {k: nc.dram_tensor(k, a.shape, mb.dt.from_np(a.dtype), kind="ExternalInput").ap() for k, a in arrays.items()}
    out = nc.dram_tensor("out", (BATCH * SEQ, HID), mb.dt.float32, kind="ExternalOutput").ap()
    build(nc, out=out, **aps)
    r = run_bass_kernel_spmd(nc, [arrays], core_ids=[0])
    return r.results[0]["out"].reshape(BATCH, SEQ, HID)
```

```python
import concourse.bass as bass
from concourse import mybir
from contextlib import ExitStack

BATCH, SEQ, HID, HEADS = 4, 2048, 256, 16
HEAD = HID // HEADS
WIN = 128
GLOB = 64
GAP = SEQ // GLOB
GPW = WIN // GAP
CW = 4
CT = CW * WIN
CHUNKS = BATCH * SEQ // CT
WINS = CHUNKS * CW
WPB = SEQ // WIN
CPB = SEQ // CT
KC = HID // 128
GH = 4
NG = HEADS // GH
VW = HEAD + 1
NV = HEADS * VW
COR = NV + HEADS
RUNS = [[(0, 3), (0, 2), (0, 1)], [(0, 3), (1, 2), (2, 1)]]
NPROD = 6
SROWS = NPROD * HEAD
MPART = 3
TROWS = SROWS + MPART
SCALE = HEAD ** -0.5
EPS = 1e-5


class Chunk:

    def __init__(self, i, c):
        self.i, self.c = i, c
        self.p = c % 2

    def shift(self, d):
        return Chunk(self.i, self.c + d)

    def exists(self):
        return self.i is not None or 0 <= self.c < CHUNKS

    def is_first(self):
        return self.i is None and self.c == 0

    def number(self):
        return self.c if self.i is None else self.i * 2 + self.c

    def count(self, per_chunk, more):
        if self.i is None:
            return self.c * per_chunk + more
        assert self.c * per_chunk + more > 0
        return self.i * (2 * per_chunk) + (self.c * per_chunk + more)

    def half_count(self, per_chunk):
        if self.i is None:
            return (self.c // 2 + 1) * per_chunk
        return self.i * per_chunk + (self.c // 2 + 1) * per_chunk


def back(ch, w, d):
    q, r = divmod(w - d, CW)
    return ch.shift(q), r


def slot(un, part):
    return 2 - part if un % 2 else part


def upto(eng, sem, value):
    if isinstance(value, int) and value <= 0:
        return
    eng.wait_ge(sem, value)


LOOP_FROM, LOOP_TIMES, LAST = 3, 5, CHUNKS + 2


def walk(eng, step):
    for c in range(LOOP_FROM):
        for w in range(CW):
            step(Chunk(None, c), w)
    with eng.Fori(0, LOOP_TIMES) as i:
        for c in range(LOOP_FROM, LOOP_FROM + 2):
            for w in range(CW):
                step(Chunk(i, c), w)
    for c in range(LOOP_FROM + 2 * LOOP_TIMES, LAST):
        for w in range(CW):
            step(Chunk(None, c), w)


def build(nc, x, xT, xgT, wq, wk, wv, wo, wr, wk2, wv2, bqk, bv, bo, mu_rk, out):
    f32, bf16 = mybir.dt.float32, mybir.dt.bfloat16
    ALU, ACT, AX = mybir.AluOpType, mybir.ActivationFunctionType, mybir.AxisListType

    x_tok = x.rearrange("(n w p) f -> n p w f", w=CW, p=WIN)
    out_tok = out.rearrange("(n w p) f -> n p w f", w=CW, p=WIN)
    xT_v = xT.rearrange("(k p) (n t) -> n p k t", p=128, t=CT)
    xT_b = xT.rearrange("(k p) (b t) -> b p k t", p=128, b=BATCH)
    parts_dram = nc.dram_tensor("parts_dram", (2, 2, KC, 3, 128, CT), bf16, kind="Internal").ap()
    cor_dram = nc.dram_tensor("cor_dram", (BATCH * GLOB, COR), f32, kind="Internal").ap()
    vrest_dram = nc.dram_tensor("vrest_dram", (WINS, NV), f32, kind="Internal").ap()
    cor_v = cor_dram.rearrange("(n w r) f -> n r w f", w=CW, r=GPW)
    vrest_v = vrest_dram.rearrange("(n a w) f -> n a (w f)", a=2, w=CW // 2)

    ctx = ExitStack()
    with ctx:
        def sb(name, shape, dt=f32):
            return ctx.enter_context(nc.sbuf_tensor(name, shape, dt))

        def pb(name, shape):
            return ctx.enter_context(nc.psum_tensor(name, shape, f32))

        def sem(name):
            return ctx.enter_context(nc.semaphore(name))

        W = {k: sb("w_" + k, [128, KC, HID]) for k in ("q", "k", "v", "o", "r", "k2", "v2")}
        W_DRAM = dict(q=wq, k=wk, v=wv, o=wo, r=wr, k2=wk2, v2=wv2)
        b_col = sb("b_col", [128, 2, KC])
        bv_row = sb("bv_row", [128, HID])
        bo_row = sb("bo_row", [128, HID])
        mu = sb("mu", [128, 2, KC])
        one_mu = sb("one_mu", [128, 2, KC])
        keep = sb("keep", [128, CHUNKS])
        ident = sb("ident", [128, 128])
        ident_h = sb("ident_h", [128, 128], bf16)
        minus_half = sb("minus_half", [128, 1])
        eps = sb("eps", [128, 1])
        xT_sb = sb("xT_sb", [128, 2, KC, CT])
        x_sb = sb("x_sb", [128, CW, HID])
        cor = sb("cor", [128, 2, CW, COR])
        vrest = sb("vrest", [128, CW, NV])
        parts = sb("parts", [128, 2, 3, CT], bf16)
        rest = sb("rest", [128, 2, CT])
        stack = [[sb(f"stack{p}{k}", [128, HEADS, CT], bf16) for k in "qk"] for p in range(2)]
        va_all = sb("va_all", [128, 2, CW, NV + 32 - VW])
        va = va_all[:, :, :, 0:NV].rearrange("p a w (h d) -> p a w h d", h=HEADS)
        smax = sb("smax", [128, 2, HEADS])
        negm = sb("negm", [128, 2, HEADS])
        m_rest = sb("m_rest", [128, 2, HEADS])
        m_diff = sb("m_diff", [128, 2, HEADS])
        m_parts = sb("m_parts", [128, 2, 8, HEADS], bf16)
        mT = sb("mT", [MPART * HEADS, 2, 128], bf16)
        e_zero = sb("e_zero", [128, 2, HEADS])
        e_cor = sb("e_cor", [128, 2, HEADS])
        pT = sb("pT", [128, 2, HEADS, WIN])
        av = sb("av", [128, 2, NG * WIN])
        t_rest = sb("t_rest", [128, NV])
        t_cor = sb("t_cor", [128, NV])
        other = sb("other", [128, 2, NV])
        num = sb("num", [128, 2, HEADS, VW])
        rden = sb("rden", [128, 2, HEADS])
        att = sb("att", [128, 2, HID])
        attT = sb("attT", [128, 2, KC, WIN])
        x_bo = sb("x_bo", [128, 2, HID])
        y = sb("y", [128, 2, HID])
        st1 = sb("st1", [128, 2, 6])
        mv1 = sb("mv1", [128, 2, 2])
        ve1 = sb("ve1", [128, 2, 1])
        rs1 = sb("rs1", [128, 2, 1])
        x1 = sb("x1", [128, 8, HID])
        x1T = sb("x1T", [128, 2, KC, CT + 1])
        mix_a = sb("mix_a", [128, KC, CT])
        xk = sb("xk", [128, KC, CT])
        xr = sb("xr", [128, KC, CT])
        kact = sb("kact", [128, KC, CT])
        th = sb("th", [128, 2, HID])
        u = sb("u", [128, 2, HID])
        z = sb("z", [128, 2, HID])
        st2 = sb("st2", [128, 2, 6])
        mv2 = sb("mv2", [128, 2, 2])
        ve2 = sb("ve2", [128, 2, 1])
        rs2 = sb("rs2", [128, 2, 1])
        o_sb = sb("o_sb", [128, 2, HID])

        flat = [stack[1][k][:, :, :].rearrange("p h t -> p (h t)").bitcast(f32) for k in range(2)]
        sum_in = [flat[0][:, SEQ * k:SEQ * (k + 1)] for k in range(2)]
        xg_sb = kact[:, :, 0:HID]
        gq = kact[:, :, HID:2 * HID]
        gk = xr[:, :, 0:HID]
        k_diag = pT[:, :, :, :].rearrange("p a h t -> p (a h t)").rearrange(
            "p (g h t) -> p g h t", g=KC, h=8)
        gs2 = [flat[1][0:GLOB, GLOB * HEADS * n:GLOB * HEADS * (n + 1)] for n in range(2)]
        gs1 = [flat[1][0:GLOB, GLOB * HEADS * n:GLOB * HEADS * (n + 1)] for n in range(2, 4)]
        x1T_flat = x1T[0:GLOB, :, :, :].rearrange("p a k t -> p (a k t)")
        gc = [x1T_flat[:, GLOB * HEADS * n:GLOB * HEADS * (n + 1)] for n in range(2)]
        gcT = [a[0:GLOB, :, :].rearrange("p k t -> p (k t)") for a in (xk, mix_a)]
        gv = av[0:GLOB, :, 0:NV].rearrange("p a (h d) -> p a h d", h=HEADS)
        g_out = x_sb[0:GLOB, :, :].rearrange("p w f -> p (w f)")[:, 0:2 * COR].rearrange("p (a f) -> p a f", a=2)
        same = sb("same", [GLOB, GLOB])
        hmask = sb("hmask", [128, 8])
        xwin = sb("xwin", [128, KC, WINS])
        xbat = sb("xbat", [128, KC, BATCH])
        xrest = sb("xrest", [128, KC, WINS])
        vr_sb = sb("vr_sb", [WINS, NV])

        S = pb("S", [128, 2, 512])
        T = pb("T", [128, 2, 512])
        V = pb("V", [128, 512])
        A = pb("A", [128, 512])
        B = pb("B", [128, 512])
        C = pb("C", [128, 512])

        w_in = sem("w_in")
        xg_in = sem("xg_in")
        xT_in = [sem(f"xT_in{p}") for p in range(2)]
        x_in = [sem(f"x_in{p}") for p in range(2)]
        m_in = sem("m_in")
        rest_in = [sem(f"rest_in{p}") for p in range(2)]
        cor_in = [sem(f"cor_in{p}") for p in range(2)]
        sum_loaded = [sem(f"sum_loaded{p}") for p in range(2)]
        parts_out = sem("parts_out")
        stack_in = [sem(f"stack_in{p}") for p in range(2)]
        scratch_out = sem("scratch_out")
        y_out = [sem(f"y_out{p}") for p in range(2)]
        const_done = sem("const_done")
        ones_done = sem("ones_done")
        dve_const = sem("dve_const")
        one_mu_done = sem("one_mu_done")
        g_proj = sem("g_proj")
        g_qk = sem("g_qk")
        g_diag = [sem(f"g_diag{k}") for k in range(KC)]
        g_score = sem("g_score")
        g_vp = sem("g_vp")
        g_v = sem("g_v")
        g_max = sem("g_max")
        g_arg0 = sem("g_arg0")
        g_arg2 = sem("g_arg2")
        g_arg1 = sem("g_arg1")
        g_exp = sem("g_exp")
        g_cor = sem("g_cor")
        g_tr = sem("g_tr")
        g_cT = sem("g_cT")
        g_num = sem("g_num")
        g_row = sem("g_row")
        g_stored = [sem(f"g_stored{p}") for p in range(2)]
        x_summed = [sem(f"x_summed{k}") for k in range(KC)]
        xrest_done = sem("xrest_done")
        vr_proj = sem("vr_proj")
        vr_done = sem("vr_done")
        qk_mm = sem("qk_mm")
        v_mm = sem("v_mm")
        s_mm = sem("s_mm")
        mT_mm = sem("mT_mm")
        t_mm = sem("t_mm")
        pv_mm = sem("pv_mm")
        avT_mm = sem("avT_mm")
        attT_mm = sem("attT_mm")
        wo_mm = sem("wo_mm")
        x1T_mm = sem("x1T_mm")
        k2_mm = sem("k2_mm")
        r_mm = sem("r_mm")
        v2_mm = sem("v2_mm")
        part1 = sem("part1")
        part2 = sem("part2")
        relu_done = sem("relu_done")
        kact_done = sem("kact_done")
        mix_a_done = sem("mix_a_done")
        mT_sb = sem("mT_sb")
        exp_done = sem("exp_done")
        av_sb = sem("av_sb")
        e_done = sem("e_done")
        attT_sb = sem("attT_sb")
        x1T_sb = sem("x1T_sb")
        th_done = sem("th_done")
        rest_done = sem("rest_done")
        va_done = sem("va_done")
        smax_done = sem("smax_done")
        negm_done = sem("negm_done")
        att_done = sem("att_done")
        mv1_done = sem("mv1_done")
        x1_done = sem("x1_done")
        halo_done = sem("halo_done")
        mix_done = sem("mix_done")
        v2_used = sem("v2_used")
        mv2_done = sem("mv2_done")
        o_done = sem("o_done")
        dve_seq = sem("dve_seq")
        parts_done = sem("parts_done")
        m_diff_done = sem("m_diff_done")
        m_parts_done = sem("m_parts_done")
        other_done = sem("other_done")
        x_bo_done = sem("x_bo_done")
        rs1_done = sem("rs1_done")
        rs2_done = sem("rs2_done")
        pool_seq = sem("pool_seq")

        class Chain:

            def __init__(self, eng, semaphore):
                self.eng, self.sem, self.n = eng, semaphore, 0

            def link(self, ins):
                self.n += 1
                ins.then_inc(self.sem, 1)

            def after(self):
                self.eng.wait_ge(self.sem, self.n)

            def restart(self):
                if self.n:
                    self.after()
                    self.eng.sem_clear(self.sem)
                    self.n = 0

        N_FIRST, N_REST = 6, 6
        block = ctx.enter_context(nc.Block())

        @block.sync
        def _(sp):
            sp.dma_start(xg_sb, xgT.rearrange("(k p) t -> p k t", p=128)).then_inc(xg_in, 16)
            for k in ("q", "k", "v"):
                sp.dma_start(W[k][:, :, :], W_DRAM[k].rearrange("(k p) n -> p k n", p=128)).then_inc(xg_in, 16)
            sp.dma_start(b_col[:, :, :], bqk).then_inc(xg_in, 16)
            sp.dma_start(bv_row[:, :], bv.partition_broadcast(128)).then_inc(xg_in, 16)

            def load_xT(ch):
                if not ch.exists():
                    return
                upto(sp, v_mm, ch.count(CW, -CW))
                sp.dma_start(xT_sb[:, ch.p, :, :], xT_v[bass.ds(ch.number(), 1)].rearrange("o p k t -> p (o k) t")
                             ).then_inc(xT_in[ch.p], 16)

            def load_tokens(ch):
                if not ch.exists():
                    return
                upto(sp, other_done, ch.count(CW, -CW))
                n = bass.ds(ch.number(), 1)
                sp.dma_start(cor[0:WIN:GAP, ch.p, :, :], cor_v[n].rearrange("o r w f -> r (o w) f")
                             ).then_inc(cor_in[ch.p], 16)

            def load_rest(ch, half):
                if not ch.exists():
                    return
                upto(sp, other_done, ch.count(CW, -CW + 2 * (half + 1)))
                sp.dma_start(vrest[:, 2 * half:2 * half + 2, :].rearrange("p w f -> p (w f)"),
                             vrest_v[bass.ds(ch.number(), 1)].rearrange("o a f -> (o a) f")[half].partition_broadcast(128)
                             ).then_inc(rest_in[half], 16)

            def load_x(ch, half):
                upto(sp, x_bo_done, ch.count(CW, -CW + 2 * (half + 1)))
                sp.dma_start(x_sb[:, 2 * half:2 * half + 2, :],
                             x_tok[bass.ds(ch.number(), 1)].rearrange("o p w f -> p (o w) f")[:, 2 * half:2 * half + 2, :]
                             ).then_inc(x_in[half], 16)

            load_xT(Chunk(None, 0))
            for k in range(2):
                sp.dma_start(sum_in[k], xT_b[0, :, k, :]).then_inc(sum_loaded[k], 16)
            for k in ("o", "r", "k2", "v2"):
                sp.dma_start(W[k][:, :, :], W_DRAM[k].rearrange("(k p) n -> p k n", p=128)).then_inc(w_in, 16)
            sp.dma_start(mu[:, :, :], mu_rk).then_inc(w_in, 16)
            sp.dma_start(bo_row[:, :], bo.partition_broadcast(128)).then_inc(w_in, 16)

            def now(value):
                return value if isinstance(value, int) else sp.snap(sp.to_reg(value))

            def restack(m, un):
                kind, g = un % 2, un // 2
                if un == 0:
                    read_at = now(m.count(CW * NG, -CW * NG))
                split_at = now(m.count(4, un + 1))
                stored_at = now(m.count(4 * 16, 16 * (un + 1)))
                if un == 0:
                    upto(sp, t_mm, read_at)
                sp.wait_ge(parts_done, split_at)
                sp.dma_start(parts_dram[m.p, kind, g].rearrange("s p t -> p s t"), parts[:, un % 2, :, :]
                             ).then_inc(parts_out, 16)
                sp.wait_ge(parts_out, stored_at)
                pr = 0
                for s, n in RUNS[kind]:
                    sp.dma_start(stack[m.p][kind][HEAD * pr:HEAD * (pr + n), 8 * g:8 * g + 8, :],
                                 parts_dram[m.p, kind, g, s:s + n].rearrange("s (d h) t -> (s d) h t", d=HEAD)
                                 ).then_inc(stack_in[m.p], 16)
                    pr += n

            load_xT(Chunk(None, 1))

            def store_row(b):
                sp.wait_ge(g_row, b + 1)
                sp.dma_start(cor_dram[b * GLOB:(b + 1) * GLOB, :], g_out[:, b % 2, :]).then_inc(g_stored[b % 2], 16)

            for b in range(BATCH):
                restack(Chunk(None, 0), b)
                if b:
                    store_row(b - 1)
                if b + 1 < BATCH:
                    for k in range(KC):
                        sp.wait_ge(x_summed[k], b + 1)
                        sp.dma_start(sum_in[k], xT_b[b + 1, :, k, :]).then_inc(sum_loaded[k], 16)
            store_row(BATCH - 1)
            sp.wait_ge(vr_done, 1)
            sp.dma_start(vrest_dram, vr_sb[:, :]).then_inc(scratch_out, 16)
            for p in range(2):
                sp.wait_ge(g_stored[p], 16 * BATCH // 2)
            sp.wait_ge(scratch_out, 16)
            load_tokens(Chunk(None, 0))
            load_rest(Chunk(None, 0), 0)

            def store(f, fw):
                if f.exists():
                    sp.wait_ge(o_done, f.count(CW, fw + 1))
                    n = bass.ds(f.number(), 1)
                    sp.dma_start(out_tok[n].rearrange("o p w f -> p (o w) f")[:, fw, :], o_sb[:, fw % 2, :]
                                 ).then_inc(y_out[fw % 2], 16)

            def step(ch, w):
                nxt = ch.shift(1)
                if w == 1:
                    load_rest(ch, 1)
                if w == 0:
                    load_xT(ch.shift(2))
                if w % 2 == 0 and ch.exists():
                    load_x(ch, w // 2)
                if w < 2 and nxt.exists():
                    restack(nxt, 2 * w)
                store(*back(ch, w, 8))
                if w < 2 and nxt.exists():
                    restack(nxt, 2 * w + 1)
                if w == 2:
                    load_tokens(nxt)
                if w == 3:
                    load_rest(nxt, 0)

            walk(sp, step)
            for p in range(2):
                sp.wait_ge(y_out[p], 16 * CHUNKS * CW // 2)

        @block.tensor
        def _(pe):
            mm, tr = nc.tensor.matmul, nc.tensor.transpose

            def project(dst, lhs, rhs):
                for kc in range(KC):
                    last = mm(dst, lhs(kc), rhs(kc), start=(kc == 0), stop=(kc == KC - 1))
                return last

            pe.wait_ge(xg_in, 16 * N_FIRST)
            banks = [S[:, 0], S[:, 1], T[:, 0], T[:, 1]]
            for n, (k, g) in enumerate((k, g) for k in "qk" for g in range(KC)):
                project(banks[n][:, 0:HID], lambda kc: W[k][:, kc, 128 * g:128 * g + 128],
                        lambda kc: xg_sb[:, kc, :]).then_inc(g_proj, 1)

            def unit(m, un):
                kind, g = un % 2, un // 2
                if un == 0:
                    pe.wait_ge(xT_in[m.p], m.half_count(16))
                    upto(pe, va_done, m.count(CW, 0))
                else:
                    pe.wait_ge(rest_done, m.count(4, un))
                project(A[:, :], lambda kc: W["qk"[kind]][:, kc, 128 * g:128 * g + 128],
                        lambda kc: xT_sb[:, m.p, kc, :]).then_inc(qk_mm, 1)

            def v_unit(m, w):
                project(A[:, 0:HID], lambda kc: xT_sb[:, m.p, kc, WIN * w:WIN * (w + 1)],
                        lambda kc: W["v"][:, kc, :]).then_inc(v_mm, 1)

            def global_scores(b):
                tok = slice(GLOB * b, GLOB * (b + 1))
                if b:
                    pe.wait_ge(g_arg0, b)
                for g in range(KC):
                    last = mm(S[0:GLOB, g, :], gq[:, g, tok], k_diag[:, g, :, tok], start=True, stop=True)
                last.then_inc(g_score, 1)
                if b:
                    pe.wait_ge(g_v, b)
                project(V[0:GLOB, 0:HID], lambda kc: xg_sb[:, kc, tok], lambda kc: W["v"][:, kc, :]
                        ).then_inc(g_vp, 1)

            def global_numerators(b):
                pe.wait_ge(g_cor, b + 1)
                for h in range(HEADS):
                    last = tr(T[0:GLOB, h // 8, GLOB * (h % 8):GLOB * (h % 8 + 1)],
                              gc[b % 2][:, GLOB * h:GLOB * (h + 1)], ident[0:GLOB, 0:GLOB])
                last.then_inc(g_tr, 1)
                pe.wait_ge(g_cT, b + 1)
                pe.wait_ge(g_v, b + 1)
                if b:
                    pe.wait_ge(g_row, b)
                for h in range(HEADS):
                    last = mm(B[0:GLOB, VW * h:VW * (h + 1)], gcT[b % 2][:, GLOB * h:GLOB * (h + 1)],
                              gv[:, b % 2, h, :], start=True, stop=True)
                last.then_inc(g_num, 1)

            first = Chunk(None, 0)
            for b in range(BATCH):
                if b:
                    pe.wait_ge(va_done, b)
                unit(first, b)
                if b == 0:
                    pe.wait_ge(const_done, 1)
                    for k in range(KC):
                        pe.wait_ge(g_diag[k], 1)
                    pe.wait_ge(g_qk, 4)
                global_scores(b)
                pe.wait_ge(rest_done, b + 1)
                v_unit(first, b)
                if b:
                    global_numerators(b - 1)
            global_numerators(BATCH - 1)
            pe.wait_ge(xrest_done, 1)
            project(V[0:WINS, 0:HID], lambda kc: xrest[:, kc, :], lambda kc: W["v"][:, kc, :]).then_inc(vr_proj, 1)

            def scores(ch, w, g):
                if w == 0 and g == 0:
                    pe.wait_ge(stack_in[ch.p], ch.half_count(16 * 4 * len(RUNS[0])))
                upto(pe, smax_done, ch.count(CW * NG, NG * w + g - 1))
                if g == 0:
                    upto(pe, mT_sb, ch.count(CW, w))
                q, k = stack[ch.p]
                tok = slice(WIN * w, WIN * (w + 1))
                for j in range(GH):
                    h = GH * g + j
                    last = mm(S[:, g % 2, WIN * j:WIN * (j + 1)], q[0:SROWS, h, tok], k[0:SROWS, h, tok],
                              start=True, stop=True)
                last.then_inc(s_mm, 1)

            def scores_T(ch, w, g):
                if g == 0:
                    pe.wait_ge(m_in, ch.count(16 * MPART * CW, 16 * MPART * (w + 1)))
                upto(pe, exp_done, ch.count(CW * NG, NG * w + g - 1))
                q, k = stack[ch.p]
                tok = slice(WIN * w, WIN * (w + 1))
                for j in range(GH):
                    h = GH * g + j
                    last = mm(T[:, g % 2, WIN * j:WIN * (j + 1)], k[0:TROWS, h, tok], q[0:TROWS, h, tok],
                              start=True, stop=True)
                last.then_inc(t_mm, 1)

            def times_v(ch, w, g):
                pe.wait_ge(exp_done, ch.count(CW * NG, NG * w + g + 1))
                if g == 0:
                    upto(pe, av_sb, ch.count(CW, w))
                for j in range(GH):
                    h = GH * g + j
                    last = mm(V[32 * j:32 * (j + 1), WIN * g:WIN * (g + 1)], va_all[:, ch.p, w, VW * h:VW * h + 32],
                              pT[:, w % 2, h, :], start=True, stop=True)
                if g == NG - 1:
                    last.then_inc(pv_mm, 1)

            def step(ch, w):
                nxt, prev = ch.shift(1), ch.shift(-1)
                s, t = ch.exists(), back(ch, w, 1)
                o, l = back(ch, w, 2), back(ch, w, 3)
                f = back(ch, w, 7)
                f_before = back(ch, w, 8)
                if s:
                    scores(ch, w, 0)
                    scores(ch, w, 1)
                if l[0].exists():
                    pe.wait_ge(x1_done, l[0].count(CW, l[1] + 1))
                    for kc in range(KC):
                        last = tr(B[:, 128 * kc:128 * (kc + 1)],
                                  x1[:, 4 * l[0].p + l[1], 128 * kc:128 * (kc + 1)], ident[:, :])
                    last.then_inc(x1T_mm, 1)
                if nxt.exists():
                    if w < 2:
                        unit(nxt, 2 * w)
                    elif w == 2:
                        pe.wait_ge(rest_done, nxt.count(4, 4))
                        v_unit(nxt, 0)
                if s:
                    scores(ch, w, 2)
                if t[0].exists():
                    scores_T(*t, 0)
                    scores_T(*t, 1)
                if o[0].exists():
                    upto(pe, x1T_sb, o[0].count(CW, o[1]))
                    pe.wait_ge(av_sb, o[0].count(CW, o[1] + 1))
                    for g in range(NG):
                        last = tr(B[:, 128 * g:128 * (g + 1)], av[:, o[1] % 2, WIN * g:WIN * (g + 1)], ident[:, :])
                    last.then_inc(avT_mm, 1)
                if w == 3 and prev.exists():
                    pe.wait_ge(relu_done, prev.count(KC, 1))
                    project(A[:, :], lambda kc: W["k2"][:, kc, 128:256], lambda kc: xk[:, kc, :]).then_inc(k2_mm, 1)
                if s:
                    scores(ch, w, 3)
                if nxt.exists():
                    if w < 2:
                        unit(nxt, 2 * w + 1)
                    elif w == 2:
                        pe.wait_ge(va_done, nxt.count(CW, 1))
                        v_unit(nxt, 1)
                    else:
                        if prev.exists():
                            pe.wait_ge(relu_done, prev.count(KC, 2))
                        else:
                            pe.wait_ge(va_done, nxt.count(CW, 2))
                        v_unit(nxt, 2)
                if t[0].exists():
                    times_v(*t, 1)
                    times_v(*t, 0)
                if o[0].exists():
                    pe.wait_ge(att_done, o[0].count(CW, o[1] + 1))
                    for kc in range(KC):
                        last = tr(B[:, 128 * kc:128 * (kc + 1)], att[:, o[1] % 2, 128 * kc:128 * (kc + 1)],
                                  ident[:, :])
                    last.then_inc(attT_mm, 1)
                if t[0].exists():
                    scores_T(*t, 2)
                    scores_T(*t, 3)
                if f[0].exists():
                    if f_before[0].exists():
                        pe.wait_ge(v2_used, f_before[0].count(CW, f_before[1] + 1))
                    pe.wait_ge(mix_done, f[0].count(2, 2))
                    project(C[:, 0:HID], lambda kc: xr[:, kc, WIN * f[1]:WIN * (f[1] + 1)],
                            lambda kc: W["r"][:, kc, :]).then_inc(r_mm, 1)
                if o[0].exists():
                    pe.wait_ge(attT_sb, o[0].count(CW, o[1] + 1))
                    project(B[:, 0:HID], lambda kc: attT[:, o[1] % 2, kc, :], lambda kc: W["o"][:, kc, :]
                            ).then_inc(wo_mm, 1)
                if s:
                    pe.wait_ge(m_parts_done, ch.count(CW, w + 1))
                    tr(S[:, 0, 0:64].bitcast(bf16), m_parts[:, w % 2, :, :].rearrange("p s h -> p (s h)"),
                       ident_h[:, :]).then_inc(mT_mm, 1)
                if t[0].exists():
                    times_v(*t, 2)
                    times_v(*t, 3)
                if nxt.exists() and w == 3:
                    pe.wait_ge(va_done, nxt.count(CW, 3))
                    v_unit(nxt, 3)
                if f[0].exists():
                    pe.wait_ge(th_done, f[0].count(CW, f[1] + 1))
                    pe.wait_ge(kact_done, f[0].count(KC, KC))
                    project(C[:, 0:HID], lambda kc: kact[:, kc, WIN * f[1]:WIN * (f[1] + 1)],
                            lambda kc: W["v2"][:, kc, :]).then_inc(v2_mm, 1)
                if w == 2 and prev.exists():
                    if nxt.exists():
                        pe.wait_ge(va_done, nxt.count(CW, 2))
                    else:
                        upto(pe, relu_done, prev.count(KC, 0))
                    pe.wait_ge(mix_done, prev.count(2, 1))
                    project(A[:, :], lambda kc: W["k2"][:, kc, 0:128], lambda kc: xk[:, kc, :]).then_inc(k2_mm, 1)

            pe.wait_ge(const_done, 2)
            pe.wait_ge(ones_done, 2)
            pe.wait_ge(w_in, 16 * N_REST)
            walk(pe, step)

        @block.scalar
        def _(act):
            fn = nc.scalar.activation
            act.wait_ge(xg_in, 16 * N_FIRST)
            banks = [S[:, 0], S[:, 1], T[:, 0], T[:, 1]]
            for n in range(4):
                kind, g = n // 2, n % 2
                act.wait_ge(g_proj, n + 1)
                fn((gk if kind else gq)[:, g, :], banks[n][:, 0:HID], ACT.Identity,
                   bias=b_col[:, kind, g:g + 1]).then_inc(g_qk, 1)

            def first_part(m, un):
                kind, g = un % 2, un // 2
                act.wait_ge(qk_mm, m.count(4, un + 1))
                upto(act, parts_out, m.count(64, 16 * (un - 1)))
                fn(parts[:, un % 2, slot(un, 0), :], A[:, :], ACT.Identity, bias=b_col[:, kind, g:g + 1]).then_inc(part1, 1)

            def second_part(m, un):
                act.wait_ge(rest_done, m.count(4, un + 1))
                fn(parts[:, un % 2, slot(un, 1), :], rest[:, un % 2, :], ACT.Identity).then_inc(part2, 1)

            def global_exp(b):
                act.wait_ge(g_arg2, b + 1)
                fn(gs2[b % 2], gs2[b % 2], ACT.Exp, scale=SCALE)
                act.wait_ge(g_arg1, b + 1)
                fn(gs1[b % 2], gs1[b % 2], ACT.Exp, scale=SCALE).then_inc(g_exp, 1)

            def global_transposed(b):
                act.wait_ge(g_tr, b + 1)
                if b >= 2:
                    act.wait_ge(g_num, b - 1)
                fn(gcT[b % 2], T[0:GLOB, :, :].rearrange("p a t -> p (a t)"), ACT.Copy).then_inc(g_cT, 1)

            for b in range(BATCH):
                first_part(Chunk(None, 0), b)
                second_part(Chunk(None, 0), b)
                if b:
                    global_transposed(b - 1)
                global_exp(b)
                act.wait_ge(sum_loaded[1], 16 * (b + 1))
                for w in range(WPB):
                    tok = sum_in[1][:, WIN * w:WIN * (w + 1)]
                    last = fn(tok, tok, ACT.Identity, accum_out=xwin[:, 1, WPB * b + w:WPB * b + w + 1])
                last.then_inc(x_summed[1], 1)
            global_transposed(BATCH - 1)

            def share_of_before(ch, which):
                for kc in range(KC):
                    fn(mix_a[:, kc, :], x1T[:, ch.p, kc, 0:CT], ACT.Identity,
                       scale=one_mu[:, which, kc:kc + 1]).then_inc(mix_a_done, 1)

            def relu(ch, half):
                act.wait_ge(k2_mm, ch.count(KC, half + 1))
                upto(act, v2_mm, ch.count(CW, 0))
                fn(kact[:, half, :], A[:, :], ACT.Relu).then_inc(relu_done, 1)

            def square(ch, half):
                act.wait_ge(relu_done, ch.count(KC, half + 1))
                fn(kact[:, half, :], kact[:, half, :], ACT.Square).then_inc(kact_done, 1)

            act.wait_ge(one_mu_done, 1)

            def step(ch, w):
                nxt, prev = ch.shift(1), ch.shift(-1)
                s, t = ch.exists(), back(ch, w, 1)
                o, l = back(ch, w, 2), back(ch, w, 3)
                f = back(ch, w, 7)

                def exps(g):
                    act.wait_ge(t_mm, t[0].count(CW * NG, NG * t[1] + g + 1))
                    if g == 0:
                        upto(act, pv_mm, t[0].count(CW, t[1] - 1))
                    fn(pT[:, t[1] % 2, GH * g:GH * (g + 1), :], T[:, g % 2, :].rearrange("p (h q) -> p h q", h=GH),
                       ACT.Exp, scale=SCALE).then_inc(exp_done, 1)
                if l[0].exists():
                    act.wait_ge(x1T_mm, l[0].count(CW, l[1] + 1))
                    if l[1] == 0:
                        upto(act, mix_done, l[0].count(2, -2))
                    fn(x1T[:, l[0].p, :, 1 + WIN * l[1]:1 + WIN * (l[1] + 1)],
                       B[:, 0:HID].rearrange("p (k t) -> p k t", k=KC), ACT.Copy).then_inc(x1T_sb, 1)
                if nxt.exists() and w < 2:
                    first_part(nxt, 2 * w)
                if t[0].exists():
                    exps(0)
                if w == 3 and prev.exists():
                    square(prev, 0)
                    relu(prev, 1)
                if t[0].exists():
                    exps(1)
                if w == 2 and prev.exists():
                    act.wait_ge(halo_done, prev.count(1, 1))
                    upto(act, mix_done, prev.count(2, 0))
                    share_of_before(prev, 1)
                if nxt.exists() and w < 2:
                    second_part(nxt, 2 * w)
                    first_part(nxt, 2 * w + 1)
                if w == 3 and prev.exists():
                    square(prev, 1)
                if o[0].exists():
                    act.wait_ge(attT_mm, o[0].count(CW, o[1] + 1))
                    fn(attT[:, o[1] % 2, :, :], B[:, 0:HID].rearrange("p (k t) -> p k t", k=KC), ACT.Copy
                       ).then_inc(attT_sb, 1)
                if t[0].exists():
                    exps(2)
                    exps(3)
                if s:
                    act.wait_ge(m_diff_done, ch.count(CW, w + 1))
                    upto(act, other_done, ch.count(CW, w - 1))
                    fn(e_zero[:, w % 2, :], negm[:, w % 2, :], ACT.Exp, scale=SCALE)
                    fn(e_cor[:, w % 2, :], m_diff[:, w % 2, :], ACT.Exp, scale=SCALE).then_inc(e_done, 1)
                if nxt.exists() and w < 2:
                    second_part(nxt, 2 * w + 1)
                if f[0].exists():
                    act.wait_ge(r_mm, f[0].count(CW, f[1] + 1))
                    upto(act, v2_used, f[0].count(CW, f[1] - 1))
                    fn(th[:, f[1] % 2, :], C[:, 0:HID], ACT.Tanh, scale=0.5).then_inc(th_done, 1)
                if w == 2 and prev.exists():
                    act.wait_ge(mix_done, prev.count(2, 1))
                    share_of_before(prev, 0)
                if s:
                    act.wait_ge(mT_mm, ch.count(CW, w + 1))
                    fn(mT[:, w % 2, :], S[0:MPART * HEADS, 0, 0:64].bitcast(bf16), ACT.Copy).then_inc(mT_sb, 1)
                    act.wait_ge(mT_sb, ch.count(CW, w + 1))
                    for part in range(MPART):
                        act.dma_start(stack[ch.p][0][SROWS + part:SROWS + part + 1, :, WIN * w:WIN * (w + 1)],
                                      mT[HEADS * part:HEADS * (part + 1), w % 2, :]).then_inc(m_in, 16)
                if t[0].exists():
                    act.wait_ge(pv_mm, t[0].count(CW, t[1] + 1))
                    upto(act, avT_mm, t[0].count(CW, t[1] - 1))
                    fn(av[:, t[1] % 2, :], V[:, :], ACT.Copy).then_inc(av_sb, 1)
                if w == 2 and prev.exists():
                    relu(prev, 0)

            walk(act, step)

        @block.vector
        def _(dve):
            v = nc.vector
            chain = Chain(dve, dve_seq)
            v.memset(va_all[:, :, :, :], 1.0).then_inc(dve_const, 1)
            v.memset(cor[:, :, :, :], 0.0).then_inc(dve_const, 1)
            v.memset(gv[:, :, :, :], 1.0).then_inc(dve_const, 1)
            v.memset(vr_sb[:, :], float(SEQ - WIN)).then_inc(dve_const, 1)
            v.memset(keep[:, :], 1.0).then_inc(dve_const, 1)
            dve.wait_ge(dve_const, 5)
            v.memset(keep[:, 0:CHUNKS:CPB], 0.0).then_inc(dve_const, 1)
            dve.wait_ge(dve_const, 6)
            dve.wait_ge(const_done, 1)
            v.tensor_reduce(hmask[:, :], ident[:, :].rearrange("p (d h) -> p h d", h=8), AX.X, ALU.add
                            ).then_inc(dve_const, 1)
            dve.wait_ge(dve_const, 7)
            dve.wait_ge(g_qk, 3)
            v.tensor_tensor(k_diag[:, 0, :, :], gk[:, 0, :].unsqueeze(1).broadcast_to([128, 8, HID]),
                            hmask[:, :].unsqueeze(2).broadcast_to([128, 8, HID]), ALU.mult).then_inc(g_diag[0], 1)

            def rest_of(m, un):
                kind, g = un % 2, un // 2
                dve.wait_ge(part1, m.count(4, un + 1))
                upto(dve, parts_done, m.count(4, un - 1))
                v.scalar_tensor_tensor(rest[:, un % 2, :], A[:, :], b_col[:, kind, g:g + 1],
                                       parts[:, un % 2, slot(un, 0), :],
                                       ALU.add, ALU.subtract).then_inc(rest_done, 1)

            def v_out(m, w):
                dve.wait_ge(v_mm, m.count(CW, w + 1))
                upto(dve, pv_mm, m.count(CW, -2 * CW + w + 1))
                v.tensor_tensor(va[:, m.p, w, :, 0:HEAD], A[:, 0:HID].rearrange("p (h d) -> p h d", h=HEADS),
                                bv_row[:, :].rearrange("p (h d) -> p h d", h=HEADS), ALU.add).then_inc(va_done, 1)

            def global_args(b):
                p = b % 2
                row = g_out[:, p, NV:COR]
                dve.wait_ge(g_score, b + 1)
                if b >= 2:
                    dve.wait_ge(g_stored[p], 16 * (b // 2))
                    dve.wait_ge(g_cor, b - 1)
                sc = S[0:GLOB, :, :].rearrange("p a (h t) -> p (a h) t", t=GLOB)
                s2 = gs2[p].rearrange("p (h t) -> p h t", t=GLOB)
                s1 = gs1[p].rearrange("p (h t) -> p h t", t=GLOB)
                blk = same[:, :].unsqueeze(1).broadcast_to([GLOB, HEADS, GLOB])
                chain.link(v.scalar_tensor_tensor(s2, blk, 1.0, sc, ALU.add, ALU.mult))
                v.tensor_tensor(s1, blk, sc, ALU.mult).then_inc(g_arg0, 1)
                chain.after()
                chain.link(v.tensor_reduce(row, s2, AX.X, ALU.max, negate=True))
                chain.after()
                v.tensor_scalar(row, row, 0.0, None, ALU.min).then_inc(g_max, 1)
                dve.wait_ge(g_max, b + 1)
                v.tensor_tensor(s2, s2, row.unsqueeze(2).broadcast_to([GLOB, HEADS, GLOB]), ALU.add
                                ).then_inc(g_arg2, 1)
                dve.wait_ge(g_vp, b + 1)
                if b >= 2:
                    dve.wait_ge(g_num, b - 1)
                v.tensor_tensor(gv[:, p, :, 0:HEAD], V[0:GLOB, 0:HID].rearrange("p (h d) -> p h d", h=HEADS),
                                bv_row[0:GLOB, :].rearrange("p (h d) -> p h d", h=HEADS), ALU.add).then_inc(g_v, 1)

            def global_row(b):
                dve.wait_ge(g_num, b + 1)
                v.tensor_copy(g_out[:, b % 2, 0:NV], B[0:GLOB, 0:NV]).then_inc(g_row, 1)

            for b in range(BATCH):
                rest_of(Chunk(None, 0), b)
                global_args(b)
                v_out(Chunk(None, 0), b)
                dve.wait_ge(sum_loaded[0], 16 * (b + 1))
                v.tensor_reduce(xwin[:, 0, WPB * b:WPB * (b + 1)],
                                sum_in[0].rearrange("p (w t) -> p w t", t=WIN), AX.X, ALU.add
                                ).then_inc(x_summed[0], 1)
                if b:
                    global_row(b - 1)
            global_row(BATCH - 1)
            for k in range(KC):
                dve.wait_ge(x_summed[k], BATCH)
            xw = xwin[:, :, :].rearrange("p k (b w) -> p k b w", w=WPB)
            chain.link(v.tensor_reduce(xbat[:, :, :], xw, AX.X, ALU.add))
            chain.after()
            v.tensor_tensor(xrest[:, :, :].rearrange("p k (b w) -> p k b w", w=WPB),
                            xbat[:, :, :].unsqueeze(3).broadcast_to([128, KC, BATCH, WPB]), xw, ALU.subtract
                            ).then_inc(xrest_done, 1)
            dve.wait_ge(vr_proj, 1)
            v.scalar_tensor_tensor(vr_sb[:, :].rearrange("p (h d) -> p h d", h=HEADS)[:, :, 0:HEAD],
                                   bv_row[0:WINS, :].rearrange("p (h d) -> p h d", h=HEADS), float(SEQ - WIN),
                                   V[0:WINS, 0:HID].rearrange("p (h d) -> p h d", h=HEADS),
                                   ALU.mult, ALU.add).then_inc(vr_done, 1)
            dve.wait_ge(w_in, 16 * N_REST)
            v.tensor_scalar(one_mu[:, :, :], mu[:, :, :], -1.0, 1.0, ALU.mult, ALU.add).then_inc(one_mu_done, 1)

            def normalise(ch, w):
                if not ch.exists():
                    return
                p = w % 2
                dve.wait_ge(rs2_done, ch.count(CW, w + 1))
                if ch.i is not None or ch.c * CW + w >= 2:
                    dve.wait_ge(y_out[p], ch.count(32, 16 * (w // 2)))
                v.tensor_scalar(o_sb[:, p, :], z[:, p, :], mv2[:, p, 0:1], rs2[:, p, :],
                                ALU.subtract, ALU.mult).then_inc(o_done, 1)

            def step(ch, w):
                if w == 0:
                    chain.restart()
                nxt, prev = ch.shift(1), ch.shift(-1)
                s = ch.exists()
                o = back(ch, w, 2)
                f, g = back(ch, w, 7), back(ch, w, 8)
                wp, op, fp, gp = w % 2, o[1] % 2, f[1] % 2, g[1] % 2

                def maximum(g):
                    dve.wait_ge(s_mm, ch.count(CW * NG, NG * w + g + 1))
                    v.tensor_reduce(smax[:, wp, GH * g:GH * (g + 1)],
                                    S[:, g % 2, :].rearrange("p (h k) -> p h k", h=GH), AX.X, ALU.max,
                                    negate=True).then_inc(smax_done, 1)
                if s:
                    maximum(0)
                if g[0].exists():
                    dve.wait_ge(v2_used, g[0].count(CW, g[1] + 1))
                    chain.link(v.scalar_tensor_tensor(z[:, gp, :], u[:, gp, :], 0.5, x1[:, 4 * g[0].p + g[1], :],
                                                      ALU.mult, ALU.add))
                if s:
                    maximum(1)
                if g[0].exists():
                    chain.after()
                    chain.link(v.bn_stats(st2[:, gp, :], z[:, gp, :]))
                    chain.after()
                    v.bn_aggr(mv2[:, gp, :], st2[:, gp, :]).then_inc(mv2_done, 1)
                if nxt.exists():
                    if w < 2:
                        rest_of(nxt, 2 * w)
                    elif w == 2:
                        v_out(nxt, 0)
                if w == 2 and prev.exists():
                    dve.wait_ge(x1T_sb, prev.count(CW, CW))
                    if not prev.is_first():
                        n = prev.number()
                        k = keep[:, n:n + 1] if isinstance(n, int) else keep[:, bass.ds(n, 1)]
                        v.tensor_scalar(x1T[:, prev.p, :, 0], x1T[:, 1 - prev.p, :, CT], k, None, ALU.mult
                                        ).then_inc(halo_done, 1)
                    else:
                        v.memset(x1T[:, prev.p, :, 0:1], 0.0).then_inc(halo_done, 1)
                if o[0].exists():
                    dve.wait_ge(avT_mm, o[0].count(CW, o[1] + 1))
                    dve.wait_ge(other_done, o[0].count(CW, o[1] + 1))
                    chain.link(v.tensor_tensor(num[:, op, :, :],
                                               B[:, :].rearrange("p (h d) -> p h d", h=HEADS)[:, :, 0:VW],
                                               other[:, op, :].rearrange("p (h d) -> p h d", h=HEADS), ALU.add))
                    chain.after()
                    chain.link(v.reciprocal(rden[:, op, :], num[:, op, :, HEAD]))
                    chain.after()
                    v.tensor_tensor(att[:, op, :].rearrange("p (h d) -> p h d", h=HEADS), num[:, op, :, 0:HEAD],
                                    rden[:, op, :].unsqueeze(2).broadcast_to([128, HEADS, HEAD]), ALU.mult
                                    ).then_inc(att_done, 1)
                if s:
                    maximum(2)
                if w == 3 and prev.exists():
                    upto(dve, r_mm, prev.count(CW, 0))
                    for kc in range(KC):
                        dve.wait_ge(mix_a_done, prev.count(2 * KC, KC + kc + 1))
                        last = v.scalar_tensor_tensor(xr[:, kc, :], x1T[:, prev.p, kc, 1:CT + 1],
                                                      mu[:, 0, kc:kc + 1], mix_a[:, kc, :], ALU.mult, ALU.add)
                    last.then_inc(mix_done, 1)
                if s:
                    maximum(3)
                    if w == 0:
                        dve.wait_ge(cor_in[ch.p], ch.half_count(16))
                    dve.wait_ge(smax_done, ch.count(CW * NG, NG * (w + 1)))
                    upto(dve, e_done, ch.count(CW, w - 1))
                    upto(dve, m_parts_done, ch.count(CW, w - 1))
                    v.tensor_tensor(negm[:, wp, :], smax[:, wp, :], cor[:, ch.p, w, NV:COR], ALU.min
                                    ).then_inc(negm_done, 1)
                if w == 2 and prev.exists():
                    for kc in range(KC):
                        dve.wait_ge(mix_a_done, prev.count(2 * KC, kc + 1))
                        last = v.scalar_tensor_tensor(xk[:, kc, :], x1T[:, prev.p, kc, 1:CT + 1], mu[:, 1, kc:kc + 1],
                                                      mix_a[:, kc, :], ALU.mult, ALU.add)
                    last.then_inc(mix_done, 1)
                normalise(*g)
                if nxt.exists():
                    if w < 2:
                        rest_of(nxt, 2 * w + 1)
                    elif w == 2:
                        v_out(nxt, 1)
                    else:
                        v_out(nxt, 2)
                if o[0].exists():
                    dve.wait_ge(wo_mm, o[0].count(CW, o[1] + 1))
                    dve.wait_ge(x_bo_done, o[0].count(CW, o[1] + 1))
                    chain.link(v.tensor_tensor(y[:, op, :], B[:, 0:HID], x_bo[:, op, :], ALU.add))
                    chain.after()
                    chain.link(v.bn_stats(st1[:, op, :], y[:, op, :]))
                    chain.after()
                    v.bn_aggr(mv1[:, op, :], st1[:, op, :]).then_inc(mv1_done, 1)
                if nxt.exists() and w == 3:
                    v_out(nxt, 3)
                if o[0].exists():
                    dve.wait_ge(rs1_done, o[0].count(CW, o[1] + 1))
                    v.tensor_scalar(x1[:, 4 * o[0].p + o[1], :], y[:, op, :], mv1[:, op, 0:1], rs1[:, op, :],
                                    ALU.subtract, ALU.mult).then_inc(x1_done, 1)
                if f[0].exists():
                    dve.wait_ge(v2_mm, f[0].count(CW, f[1] + 1))
                    v.scalar_tensor_tensor(u[:, fp, :], th[:, fp, :], 1.0, C[:, 0:HID], ALU.add, ALU.mult
                                           ).then_inc(v2_used, 1)

            walk(dve, step)

        @block.gpsimd
        def _(pool):
            g_ = nc.gpsimd
            chain = Chain(pool, pool_seq)
            for tile, value in ((ident, 0.0), (ident_h, 0.0), (same, 1.0), (m_parts, 0.0)):
                chain.link(g_.memset(tile[:], value))
            chain.after()
            for tile in (ident, ident_h):
                g_.affine_select(out=tile[:, :], in_=tile[:, :], compare_op=ALU.not_equal, fill=1.0, base=0,
                                 pattern=[[-1, 128]], channel_multiplier=1)
            s3 = same[:, :].rearrange("p (w r) -> p w r", r=GPW)
            chain.link(g_.affine_select(out=s3, in_=s3, compare_op=ALU.is_ge, fill=0.0, base=0,
                                        pattern=[[-GPW, GLOB // GPW], [0, GPW]], channel_multiplier=1))
            chain.after()
            g_.affine_select(out=s3, in_=s3, compare_op=ALU.is_ge, fill=0.0, base=GPW - 1,
                             pattern=[[GPW, GLOB // GPW], [0, GPW]], channel_multiplier=-1).then_inc(const_done, 1)
            g_.memset(minus_half[:, :], -0.5)
            g_.memset(eps[:, :], EPS).then_inc(const_done, 1)
            pool.wait_ge(const_done, 2)

            def split(m, un):
                pool.wait_ge(part2, m.count(4, un + 1))
                g_.tensor_tensor(parts[:, un % 2, slot(un, 2), :], rest[:, un % 2, :], parts[:, un % 2, slot(un, 1), :],
                                 ALU.subtract
                                 ).then_inc(parts_done, 1)

            pool.wait_ge(g_qk, 4)
            pool.wait_ge(dve_const, 7)
            g_.tensor_tensor(k_diag[:, 1, :, :], gk[:, 1, :].unsqueeze(1).broadcast_to([128, 8, HID]),
                             hmask[:, :].unsqueeze(2).broadcast_to([128, 8, HID]), ALU.mult).then_inc(g_diag[1], 1)

            def global_arg(b):
                pool.wait_ge(g_max, b + 1)
                s1 = gs1[b % 2].rearrange("p (h t) -> p h t", t=GLOB)
                g_.tensor_tensor(s1, s1, g_out[:, b % 2, NV:COR].unsqueeze(2).broadcast_to([GLOB, HEADS, GLOB]), ALU.add
                                 ).then_inc(g_arg1, 1)

            for b in range(BATCH):
                split(Chunk(None, 0), b)
                global_arg(b)
                pool.wait_ge(g_exp, b + 1)
                if b >= 2:
                    pool.wait_ge(g_tr, b - 1)
                g_.tensor_tensor(gc[b % 2], gs2[b % 2], gs1[b % 2], ALU.subtract).then_inc(g_cor, 1)
            for p in range(2):
                g_.memset(stack[p][1][SROWS:TROWS, :, :], 1.0).then_inc(ones_done, 1)
            pool.wait_ge(w_in, 16 * N_REST)

            def rstd(ve, rs, mv, done):
                chain.link(g_.tensor_tensor(ve, mv, eps[:, :], ALU.add))
                chain.after()
                g_.tensor_tensor(rs, ve, minus_half[:, :], ALU.pow).then_inc(done, 1)

            def step(ch, w):
                if w == 0:
                    chain.restart()
                nxt = ch.shift(1)
                s, t = ch.exists(), back(ch, w, 1)
                o = back(ch, w, 2)
                g = back(ch, w, 8)
                wp, tp, op, gp = w % 2, t[1] % 2, o[1] % 2, g[1] % 2
                if o[0].exists():
                    if o[1] % 2 == 0:
                        pool.wait_ge(x_in[o[1] // 2], o[0].count(16, 16))
                    upto(pool, mv1_done, o[0].count(CW, o[1] - 1))
                    g_.tensor_tensor(x_bo[:, op, :], x_sb[:, o[1], :], bo_row[:, :], ALU.add
                                     ).then_inc(x_bo_done, 1)
                if g[0].exists():
                    pool.wait_ge(mv2_done, g[0].count(CW, g[1] + 1))
                    rstd(ve2[:, gp, :], rs2[:, gp, :], mv2[:, gp, 1:2], rs2_done)
                if nxt.exists() and w < 2:
                    split(nxt, 2 * w)
                if s:
                    pool.wait_ge(negm_done, ch.count(CW, w + 1))
                    upto(pool, e_done, ch.count(CW, w - 1))
                    upto(pool, mT_mm, ch.count(CW, w - 1))
                    g_.tensor_tensor(m_diff[:, wp, :], negm[:, wp, :], cor[:, ch.p, w, NV:COR], ALU.subtract
                                     ).then_inc(m_diff_done, 1)
                    chain.link(g_.tensor_copy(m_parts[:, wp, 0, :], negm[:, wp, :]))
                    chain.after()
                    chain.link(g_.tensor_tensor(m_rest[:, wp, :], negm[:, wp, :], m_parts[:, wp, 0, :], ALU.subtract))
                    chain.after()
                    chain.link(g_.tensor_copy(m_parts[:, wp, 1, :], m_rest[:, wp, :]))
                    chain.after()
                    g_.tensor_tensor(m_parts[:, wp, 2, :], m_rest[:, wp, :], m_parts[:, wp, 1, :], ALU.subtract
                                     ).then_inc(m_parts_done, 1)
                if o[0].exists():
                    pool.wait_ge(mv1_done, o[0].count(CW, o[1] + 1))
                    rstd(ve1[:, op, :], rs1[:, op, :], mv1[:, op, 1:2], rs1_done)
                if t[0].exists():
                    pool.wait_ge(e_done, t[0].count(CW, t[1] + 1))
                    if t[1] % 2 == 0:
                        pool.wait_ge(rest_in[t[1] // 2], t[0].count(16, 16))
                    if t[1] == 0:
                        pool.wait_ge(cor_in[t[0].p], t[0].half_count(16))
                    h3 = "p (h d) -> p h d"
                    ez = e_zero[:, tp, :].unsqueeze(2).broadcast_to([128, HEADS, VW])
                    ec = e_cor[:, tp, :].unsqueeze(2).broadcast_to([128, HEADS, VW])
                    chain.link(g_.tensor_tensor(t_rest[:, :].rearrange(h3, h=HEADS),
                                                vrest[:, t[1], :].rearrange(h3, h=HEADS), ez, ALU.mult))
                    chain.link(g_.tensor_tensor(t_cor[:, :].rearrange(h3, h=HEADS),
                                                cor[:, t[0].p, t[1], 0:NV].rearrange(h3, h=HEADS), ec, ALU.mult))
                    chain.after()
                    if nxt.exists() and w < 2:
                        split(nxt, 2 * w + 1)
                    chain.after()
                    upto(pool, att_done, t[0].count(CW, t[1] - 1))
                    g_.tensor_tensor(other[:, tp, :], t_rest[:, :], t_cor[:, :], ALU.add).then_inc(other_done, 1)
                elif nxt.exists() and w < 2:
                    split(nxt, 2 * w + 1)

            walk(pool, step)


def kernel(L0_attn_x, L0_attn_wq, L0_attn_bq, L0_attn_wk, L0_attn_bk, L0_attn_wv, L0_attn_bv, L0_attn_wo, L0_attn_bo,
           L0_ffn_W_r, L0_ffn_W_k, L0_ffn_W_v, L0_ffn_mu_r, L0_ffn_mu_k):
    import numpy as np
    import concourse.bacc as bacc
    from concourse import mybir as mb
    from concourse.bass_utils import run_bass_kernel_spmd

    x = np.ascontiguousarray(L0_attn_x).reshape(BATCH * SEQ, HID)
    t = lambda a: np.ascontiguousarray(np.asarray(a).T)
    columns = lambda a, b: np.ascontiguousarray(np.stack([np.asarray(v).reshape(KC, 128).T for v in (a, b)], 1))
    order = np.arange(HID).reshape(KC, 8, HEAD).transpose(0, 2, 1).ravel()
    arrays = {
        "x": x, "xT": t(x), "xgT": t(x[::GAP]),
        "wq": t(np.asarray(L0_attn_wq)[order]), "wk": t(np.asarray(L0_attn_wk)[order]),
        "wv": t(L0_attn_wv), "wo": t(L0_attn_wo),
        "wr": t(L0_ffn_W_r), "wk2": t(L0_ffn_W_k), "wv2": t(L0_ffn_W_v),
        "bqk": columns(np.asarray(L0_attn_bq)[order], np.asarray(L0_attn_bk)[order]), "bv": np.asarray(L0_attn_bv),
        "bo": np.asarray(L0_attn_bo), "mu_rk": columns(L0_ffn_mu_r, L0_ffn_mu_k),
    }
    nc = bacc.Bacc("TRN2", target_bir_lowering=False, num_devices=1)
    aps = {k: nc.dram_tensor(k, a.shape, mb.dt.from_np(a.dtype), kind="ExternalInput").ap() for k, a in arrays.items()}
    out = nc.dram_tensor("out", (BATCH * SEQ, HID), mb.dt.float32, kind="ExternalOutput").ap()
    build(nc, out=out, **aps)
    r = run_bass_kernel_spmd(nc, [arrays], core_ids=[0])
    return r.results[0]["out"].reshape(BATCH, SEQ, HID)
```
